# Optimizing a Trainium2 kernel written in Bass

```python
import numpy as np
import jax
import jax.numpy as jnp

def _softmax(x, axis=-1):
    return jax.nn.softmax(x, axis=axis)

def _gelu(x):
    return jax.nn.gelu(x, approximate=True)

def _silu(x):
    return jax.nn.silu(x)

def _sigmoid(x):
    return jax.nn.sigmoid(x)

def _layernorm(x, axis=-1, eps=1e-05):
    m = jnp.mean(x, axis=axis, keepdims=True)
    v = jnp.var(x, axis=axis, keepdims=True)
    return (x - m) / jnp.sqrt(v + eps)

def _scatter_add(tgt, idx, src, axis=0):
    return tgt.at[idx].add(src)

def _segment_sum(src, seg, n):
    return jax.ops.segment_sum(src, seg, n)
kernel_name = 'mk_seq_preln_d1_jaxref_r2_aa6592'

def setup_inputs(seed: int=0):
    np.random.seed(seed)
    _w = jnp.asarray

    def _L0_attn_setup():
        import jax, jax.numpy as jnp
        import numpy as np
        BATCH, SEQ, D_MODEL = (4, 1024, 512)
        D_STATE, D_CONV = (16, 4)

        def _silu(u):
            return u * jax.nn.sigmoid(u)
        key = jax.random.key(seed)
        ks = jax.random.split(key, 6)
        s = 0.02
        x = jax.random.normal(ks[0], (BATCH, SEQ, D_MODEL), jnp.float32)
        in_proj_w = jax.random.normal(ks[1], (2 * D_MODEL, D_MODEL), jnp.float32) * s
        conv_w = jax.random.normal(ks[2], (D_MODEL, D_CONV), jnp.float32) * s
        conv_b = jax.random.normal(ks[3], (D_MODEL,), jnp.float32) * s
        x_proj_w = jax.random.normal(ks[4], (2 * D_STATE + 1, D_MODEL), jnp.float32) * s
        A_log = jnp.log(jnp.broadcast_to(jnp.arange(1, D_STATE + 1, dtype=jnp.float32), (D_MODEL, D_STATE)))
        D_param = jnp.ones((D_MODEL,), jnp.float32)
        out_proj_w = jax.random.normal(ks[5], (D_MODEL, D_MODEL), jnp.float32) * s
        return {'x': x, 'in_proj_w': in_proj_w, 'conv_w': conv_w, 'conv_b': conv_b, 'x_proj_w': x_proj_w, 'A_log': A_log, 'D_param': D_param, 'out_proj_w': out_proj_w}
    _L0_attn_in = _L0_attn_setup()

    def _L0_ffn_setup():
        import jax, jax.numpy as jnp
        import numpy as np
        TOP_K = 2
        EPS = 1e-10
        key = jax.random.key(seed)
        k1, k2, k3, k4 = jax.random.split(key, 4)
        B, S, H, E = (4, 1024, 512, 8)
        tokens = jax.random.normal(k1, (B, S, H), dtype=jnp.float32)
        router_w = jax.random.normal(k2, (E, H), dtype=jnp.float32) * (1.0 / np.sqrt(H))
        router_b = jax.random.normal(k3, (E,), dtype=jnp.float32) * 0.01
        expert_weights = jax.random.normal(k4, (E, H, H), dtype=jnp.float32) * (1.0 / np.sqrt(H))
        return {'tokens': tokens, 'router_w': router_w, 'router_b': router_b, 'expert_weights': expert_weights}
    _L0_ffn_in = _L0_ffn_setup()
    _d = {'L0_attn_x': _L0_attn_in['x'], 'L0_attn_in_proj_w': _L0_attn_in['in_proj_w'], 'L0_attn_conv_w': _L0_attn_in['conv_w'], 'L0_attn_conv_b': _L0_attn_in['conv_b'], 'L0_attn_x_proj_w': _L0_attn_in['x_proj_w'], 'L0_attn_A_log': _L0_attn_in['A_log'], 'L0_attn_D_param': _L0_attn_in['D_param'], 'L0_attn_out_proj_w': _L0_attn_in['out_proj_w'], 'L0_ffn_router_w': _L0_ffn_in['router_w'], 'L0_ffn_router_b': _L0_ffn_in['router_b'], 'L0_ffn_expert_weights': _L0_ffn_in['expert_weights']}
    _x0 = _d['L0_attn_x']
    _d['L0_attn_x'] = jax.random.normal(jax.random.fold_in(jax.random.key(seed), 1), (8, 1024, 512), dtype=_x0.dtype)
    del _x0
    return _d

def reference(L0_attn_x, L0_attn_in_proj_w, L0_attn_conv_w, L0_attn_conv_b, L0_attn_x_proj_w, L0_attn_A_log, L0_attn_D_param, L0_attn_out_proj_w, L0_ffn_router_w, L0_ffn_router_b, L0_ffn_expert_weights):

    def _L0_attn_ref(x, in_proj_w, conv_w, conv_b, x_proj_w, A_log, D_param, out_proj_w):
        import jax, jax.numpy as jnp
        import numpy as np
        BATCH, SEQ, D_MODEL = (4, 1024, 512)
        D_STATE, D_CONV = (16, 4)

        def _silu(u):
            return u * jax.nn.sigmoid(u)
        seq_len = x.shape[1]
        d_state = A_log.shape[1]
        xz = jnp.einsum('bld,ed->ble', x, in_proj_w)
        x_ssm, z = jnp.split(xz, 2, axis=-1)
        xpad = jnp.pad(x_ssm, ((0, 0), (D_CONV - 1, 0), (0, 0)))
        x_conv = conv_b
        acc = jnp.zeros_like(x_ssm)
        for k in range(D_CONV):
            acc = acc + xpad[:, k:k + seq_len, :] * conv_w[:, k]
        x_conv = _silu(acc + conv_b)
        ssm_params = jnp.einsum('bld,ed->ble', x_conv, x_proj_w)
        Bm = ssm_params[..., :d_state]
        Cm = ssm_params[..., d_state:2 * d_state]
        delta = jax.nn.softplus(ssm_params[..., -1:])
        A = -jnp.exp(A_log)

        def step(h, inp):
            xt, Bt, Ct, dt = inp
            dA = jnp.exp(dt[:, :, None] * A[None])
            h = dA * h + dt[:, :, None] * Bt[:, None, :] * xt[:, :, None]
            y = jnp.einsum('bdn,bn->bd', h, Ct)
            return (h, y)
        h0 = jnp.zeros((x.shape[0], x.shape[2], d_state), x.dtype)
        xs = (jnp.swapaxes(x_conv, 0, 1), jnp.swapaxes(Bm, 0, 1), jnp.swapaxes(Cm, 0, 1), jnp.swapaxes(delta, 0, 1))
        _, ys = jax.lax.scan(step, h0, xs)
        y = jnp.swapaxes(ys, 0, 1)
        y = y + D_param * x_conv
        y = y * _silu(z)
        return jnp.einsum('bld,ed->ble', y, out_proj_w)

    def _L0_ffn_ref(tokens, router_w, router_b, expert_weights):
        import jax, jax.numpy as jnp
        import numpy as np
        TOP_K = 2
        EPS = 1e-10
        B, S, H = tokens.shape
        E = expert_weights.shape[0]
        logits = jnp.einsum('bsh,eh->bse', tokens, router_w) + router_b
        probs = jax.nn.softmax(logits, axis=-1)
        top_p, top_i = jax.lax.top_k(probs, TOP_K)
        w = top_p / (jnp.sum(top_p, axis=-1, keepdims=True) + EPS)
        x = tokens.reshape(-1, H)
        idx = top_i.reshape(-1, TOP_K)
        wf = w.reshape(-1, TOP_K)
        y_all = jnp.einsum('nh,ehd->ned', x, expert_weights)
        y_k = jnp.take_along_axis(y_all, idx[:, :, None], axis=1)
        out = jnp.einsum('nk,nkh->nh', wf, y_k)
        acc = jnp.clip(jnp.sum(wf, axis=-1), EPS, None)
        out = (out / acc[:, None]).reshape(B, S, H)
        scale = 1.0 + jnp.sum(w, axis=-1, keepdims=True) * EPS
        return out * scale
    x = L0_attn_x
    x = x + _L0_attn_ref(_layernorm(x, axis=-1), L0_attn_in_proj_w, L0_attn_conv_w, L0_attn_conv_b, L0_attn_x_proj_w, L0_attn_A_log, L0_attn_D_param, L0_attn_out_proj_w)
    x = x + _L0_ffn_ref(_layernorm(x, axis=-1), L0_ffn_router_w, L0_ffn_router_b, L0_ffn_expert_weights)
    return x

_drawn_inputs = setup_inputs


def setup_inputs(seed=0):
    import zlib

    import numpy as np

    out = dict(_drawn_inputs(seed))
    spreads = {'L0_attn_D_param': (1.0, 0.6)}
    factors = {'L0_attn_in_proj_w': 2.886,
     'L0_attn_conv_w': 3.533,
     'L0_attn_conv_b': 3.38,
     'L0_attn_x_proj_w': 8.0,
     'L0_attn_A_log': 8.0,
     'L0_attn_out_proj_w': 2.727}
    for name, (base, spread) in spreads.items():
        noise = np.random.default_rng([zlib.crc32(name.encode()), seed]).standard_normal(out[name].shape)
        drawn = base * np.exp(spread * noise) if base else spread * noise
        out[name] = jnp.asarray(drawn.astype(out[name].dtype))
    for name, factor in factors.items():
        out[name] = (out[name] * factor).astype(out[name].dtype)
    return out
```

```python
import concourse.bass as bass
from concourse import mybir
from contextlib import ExitStack



def mamba_moe_kernel(nc, x, in_w, conv_w, conv_b, xp_w, a_log, d_param, out_w,
                     router_w, router_b, expert_w, out):
    fp32 = mybir.dt.float32
    u32 = mybir.dt.uint32
    ALU = mybir.AluOpType
    ACT = mybir.ActivationFunctionType

    P = 128
    TOKENS, D = x.shape
    SEQ = 1024
    T = 512
    Q = T // P
    C = D // P
    N = a_log.shape[1]
    TAPS = conv_w.shape[1]
    E = expert_w.shape[0]
    BLOCKS = TOKENS // T
    BATCHES = TOKENS // SEQ
    LN_EPS = 1e-5
    EPS = 1e-10
    ROWS = 4
    UR = 4
    M = 2 * C

    prep = {n: [] for n in range(N)}
    post = {n: [] for n in range(N)}
    prep[0] += [("load_x", 0), ("load_x", 1)]
    prep[3] += [("norm_stat", 0), ("norm_rstd", 0), ("norm_stat", 1), ("norm_rstd", 1),
                ("norm_apply", 0), ("norm_apply", 1), ("norm_T", 0), ("norm_T", 1),
                ("norm_evict", 0), ("norm_evict", 1), ("load_x", 2), ("load_x", 3)]
    prep[3] += [("norm_stat", 2), ("norm_rstd", 2), ("norm_stat", 3), ("norm_rstd", 3),
                ("norm_apply", 2), ("norm_apply", 3), ("norm_T", 2), ("norm_T", 3),
                ("norm_evict", 2), ("norm_evict", 3), ("conv_edge", 0)]
    for m in range(M):
        prep[4 + m // 2].append(("project", m))
        prep[5 + m // 2].append(("project_evict", m))
    for c in range(C):
        prep[6 + c // 2].append(("conv", c))
    prep[9] += [("silu", 0), ("dt_project", 0), ("b_project", 0)]
    prep[10] += [("dt_exp", 0), ("dt_plus", 0), ("b_scale", 0), ("b_store", 0),
                 ("c_project", 0), ("c_project", 1)]
    prep[11] += [("c_evict", 0), ("c_evict", 1)]

    post[0] += [("load_res", q) for q in range(Q)]
    post[0] += [("y_T", 0), ("y_T", 1), ("y_skip", 0), ("y_skip", 1), ("y_T", 2), ("y_T", 3),
                ("y_gate", 0), ("y_gate", 1), ("y_skip", 2), ("y_skip", 3), ("y_gate", 2), ("y_gate", 3)]
    post[1] += [("out_project", 0), ("out_project", 1), ("residual", 0), ("rstd2", 0), ("residual", 1), ("rstd2", 1)]
    post[2] += [("out_project", 2), ("norm2", 0), ("norm2_T", 0), ("residual", 2), ("rstd2", 2), ("norm2_evict", 0),
                ("out_project", 3), ("router", 0), ("residual", 3), ("rstd2", 3), ("gate_logits", 0),
                ("gate_exp", 0), ("gate_top", 0), ("gate_weights", 0)]
    units = [(q, e) for q in range(Q) for e in range(E)]
    per_slot = [0, 0, 0, 1, 1, 1, 1, 3, 3, 2, 3, 3, 3, 3, 4, 4]
    head = {1: 4, 2: 9, 3: 12}
    run_, added_ = 0, 0
    for n in range(N):
        for q, s in head.items():
            if s == n:
                post[n] += [("expert_add", i) for i in range(added_, run_)]
                added_ = run_
                post[n] += [("norm2", q), ("norm2_T", q), ("norm2_evict", q), ("router", q), ("gate_logits", q),
                            ("gate_exp", q), ("gate_top", q), ("gate_weights", q)]
        for _ in range(per_slot[n]):
            if run_ - added_ == 2:
                post[n].append(("expert_add", added_))
                added_ += 1
            post[n].append(("expert", run_))
            run_ += 1
    post[N - 1] += [("expert_add", i) for i in range(added_, run_)]
    for n in range(N):
        steps = []
        for s in post[n]:
            steps.append(s)
            if s[0] == "expert_add" and units[s[1]][1] == E - 1:
                steps.append(("store", units[s[1]][0]))
        post[n] = steps

    def spread(lists, parts):
        n = len(lists)
        return [lists[n * i // parts:n * (i + 1) // parts] for i in range(parts)]

    def iteration(scan, do_prep, do_post):
        steps = []
        for n in range(N):
            side_post = spread(post[n], C) if do_post else [[]] * C
            side_prep = spread(prep[n], C) if do_prep else [[]] * C
            tail = do_post if n == 0 else scan
            m, blk = (N - 1, -1) if n == 0 else (n - 1, 0)
            if tail:
                steps += [("h_T", m, 0, blk), ("h_T", m, 1, blk)]
            if scan:
                steps.append(("load_b", n))
            for c in range(C):
                if scan:
                    steps += [("decay", n, c), ("u", n, c), ("scan", n, c)]
                if tail:
                    steps.append(("h_sum", m, c, blk))
                    if c + 2 < Q:
                        steps.append(("h_T", m, c + 2, blk))
                if n or c == C - 1:
                    steps += side_prep[c] + side_post[c] if n else sum(side_prep, []) + sum(side_post, [])
            if scan:
                steps.append(("keep_h", n))
            elif do_prep and n >= N - 3:
                pass
        return steps

    def bank_uses(table, names):
        order, k = {}, 0
        for n in range(N):
            for s in table[n]:
                if s[0] in names:
                    order[s] = k
                    k += 1
        return order, k

    PREP_USE, PREP_USES = bank_uses(prep, ("norm_T", "project", "dt_project", "b_project", "c_project"))
    POST_USE, POST_USES = bank_uses(post, ("y_T", "out_project", "norm2_T", "router", "expert"))
    assert PREP_USES % 2 == 0 and POST_USES % 2 == 0

    ctx = ExitStack()
    with ctx:
        def sb(name, shape, dt=fp32):
            return ctx.enter_context(nc.sbuf_tensor(name, shape, dt))

        def sem(name):
            return ctx.enter_context(nc.semaphore(name))

        w_in = sb("w_in", [P, C, 2 * D])
        w_out = sb("w_out", [P, C, D])
        w_exp = sb("w_exp", [P, E, C, D])
        w_xp = sb("w_xp", [P, C, 2 * N + 1])
        w_dt = sb("w_dt", [P, C, P])
        w_router = sb("w_router", [P, C, E])
        b_router = sb("b_router", [P, E])
        w_conv = sb("w_conv", [P, C, TAPS])
        b_conv = sb("b_conv", [P, C])
        d_skip = sb("d_skip", [P, C])
        neg_a = sb("neg_a", [P, C, N])
        ident = sb("ident", [P, P])
        lane = sb("lane", [P, E])
        minus_half = sb("minus_half", [P, 1])
        minus_one = sb("minus_one", [P, 2])
        xn = sb("xn", [P, 2, D])
        stat = sb("stat", [P, Q, 6])
        mv = sb("mv", [P, Q, 2])
        veps = sb("veps", [P, Q])
        rstd = sb("rstd", [P, Q])
        xs = sb("xs", [P, C, TAPS - 1 + T])
        sp = sb("sp", [P, T])
        b_rows = sb("b_rows", [N, T])
        xc = sb("xc", [P, 2, C, T])
        sz = sb("sz", [P, 2, C, T])
        dt = sb("dt", [P, 2, T])
        ct = sb("ct", [P, 2, Q, N])
        b_ring = sb("b_ring", [P, ROWS, T])
        u = sb("u", [P, UR, T])
        h = sb("h", [P, 2, C, T])
        h_last = sb("h_last", [P, N, C])
        acc = sb("acc", [P, Q, D])
        y2 = sb("y2", [P, C, T])
        xnT = y2
        x1 = sb("x1", [P, Q, D])
        stat2 = sb("stat2", [P, Q, 6])
        mv2 = sb("mv2", [P, Q, 2])
        veps2 = sb("veps2", [P, Q])
        rstd2 = sb("rstd2", [P, Q])
        xn2 = sb("xn2", [P, D])
        xn2T = sb("xn2T", [P, 2, C, P])
        logit = sb("logit", [P, E])
        top_logit = sb("top_logit", [P, 8])
        neg_top = sb("neg_top", [P, 1])
        prob = sb("prob", [P, E])
        prob_sum = sb("prob_sum", [P, 1])
        top_prob = sb("top_prob", [P, 8])
        top_at = sb("top_at", [P, 8], u32)
        top_lane = sb("top_lane", [P, 2])
        small = sb("small", [P, 8])
        pick = sb("pick", [P, 2, E])
        gate = sb("gate", [P, 2, E])

        def bank(name):
            return ctx.enter_context(nc.psum_tensor(name, [P, 512], fp32))

        decay_bank = [bank(f"decay{i}") for i in range(2)]
        hT_bank = [bank(f"hT{i}") for i in range(2)]
        prep_bank = [bank(f"prep{i}") for i in range(2)]
        post_bank = [bank(f"post{i}") for i in range(2)]

        b_dram = nc.dram_tensor("b_scratch", [2, N, T], fp32, kind="Internal").ap()

        weights_loaded = sem("weights_loaded")
        experts_loaded = sem("experts_loaded")
        ident_zero = sem("ident_zero")
        consts_ready = sem("consts_ready")
        a_ready = sem("a_ready")
        x_loaded = [sem(f"x_loaded{i}") for i in range(2)]
        stat_half = sem("stat_half")
        stat_ready = sem("stat_ready")
        veps_ready = sem("veps_ready")
        rstd_ready = sem("rstd_ready")
        xn_ready = sem("xn_ready")
        xnT_ready = sem("xnT_ready")
        prep_full = [sem(f"prep_full{i}") for i in range(2)]
        prep_free = [sem(f"prep_free{i}") for i in range(2)]
        edge_ready = sem("edge_ready")
        xs_ready = sem("xs_ready")
        conv_tap = sem("conv_tap")
        xc_ready = sem("xc_ready")
        sz_raw = sem("sz_raw")
        sz_ready = sem("sz_ready")
        sp_step = sem("sp_step")
        dt_ready = sem("dt_ready")
        b_rows_ready = sem("b_rows_ready")
        b_stored = sem("b_stored")
        ct_ready = sem("ct_ready")
        b_loaded = [sem(f"b_loaded{i}") for i in range(ROWS)]
        skip_ready = sem("skip_ready")
        u_ready = sem("u_ready")
        decay_ready = sem("decay_ready")
        scanned = sem("scanned")
        h_kept = sem("h_kept")
        hT_ready = sem("hT_ready")
        summed = sem("summed")
        post_full = [sem(f"post_full{i}") for i in range(2)]
        post_free = [sem(f"post_free{i}") for i in range(2)]
        y_skipped = sem("y_skipped")
        y_gated = sem("y_gated")
        res_loaded = [sem(f"res_loaded{i}") for i in range(Q)]
        x1_ready = sem("x1_ready")
        stat2_half = sem("stat2_half")
        stat2_ready = sem("stat2_ready")
        veps2_ready = sem("veps2_ready")
        rstd2_ready = sem("rstd2_ready")
        xn2_ready = sem("xn2_ready")
        xn2T_ready = sem("xn2T_ready")
        gate_step = sem("gate_step")
        logits_ready = sem("logits_ready")
        prob_ready = sem("prob_ready")
        top_ready = sem("top_ready")
        weight_step = sem("weight_step")
        gate_ready = sem("gate_ready")
        added = sem("added")
        stored = [sem(f"stored{i}") for i in range(Q)]

        GATE_STEPS, WEIGHT_STEPS = 7, 10
        WEIGHT_LOADS = 9

        def wait(eng, s, value):
            if not isinstance(value, int) or value > 0:
                eng.wait_ge(s, value)

        def run(eng, steps_of):
            steps_of(-1, 1, iteration(False, True, False))
            steps_of(0, 0, iteration(True, True, False))
            if BATCHES > 1:
                with eng.Fori(0, BATCHES - 1) as b:
                    steps_of(2 * b + 1, 1, iteration(True, True, True))
                    steps_of(2 * b + 2, 0, iteration(True, True, True))
            steps_of(BLOCKS - 1, 1, iteration(True, False, True))
            steps_of(BLOCKS, 0, iteration(False, False, True))

        block = ctx.enter_context(nc.Block())

        @block.sync
        def _(sync):
            sync.dma_start(w_in[:], in_w.rearrange("(k p) n -> p k n", p=P)).then_inc(weights_loaded, 16)
            sync.dma_start(w_conv[:], conv_w.rearrange("(k p) n -> p k n", p=P)).then_inc(weights_loaded, 16)
            sync.dma_start(b_conv[:], conv_b).then_inc(weights_loaded, 16)
            sync.dma_start(d_skip[:], d_param).then_inc(weights_loaded, 16)
            sync.dma_start(neg_a[:], a_log.rearrange("(k p) n -> p k n", p=P)).then_inc(weights_loaded, 16)
            sync.dma_start(w_xp[:], xp_w.rearrange("(k p) n -> p k n", p=P)).then_inc(weights_loaded, 16)
            sync.dma_start(w_router[:], router_w.rearrange("(k p) n -> p k n", p=P)).then_inc(weights_loaded, 16)
            sync.dma_start(b_router[:], router_b.rearrange("(a n) -> a n", a=1).to_broadcast([P, E])).then_inc(weights_loaded, 16)
            sync.dma_start(w_out[:], out_w.rearrange("(k p) n -> p k n", p=P)).then_inc(weights_loaded, 16)

            def steps_of(j, par, steps):
                p, r = j + 1, j - 1
                for s in steps:
                    if s[0] == "load_x":
                        q = s[1]
                        if q >= 2:
                            wait(sync, prep_full[PREP_USE["norm_T", q - 2] % 2],
                                 p * (PREP_USES // 2) + PREP_USE["norm_T", q - 2] // 2 + 1)
                            sync.nop(nofuse=True)
                        else:
                            wait(sync, xnT_ready, Q * p)
                            sync.nop(nofuse=True)
                        sync.dma_start(xn[:, q % 2, :], x[bass.ds(p * T + q * P, P), :]).then_inc(x_loaded[q % 2], 16)
                    elif s[0] == "load_res":
                        q = s[1]
                        wait(sync, stored[q], 16 * r)
                        sync.nop(nofuse=True)
                        sync.dma_start(x1[:, q, :], x[bass.ds(r * T + q * P, P), :]).then_inc(res_loaded[q], 16)
                    elif s[0] == "b_store":
                        sync.wait_ge(b_rows_ready, p + 1)
                        sync.nop(nofuse=True)
                        sync.dma_start(b_dram[1 - par], b_rows[:]).then_inc(b_stored, 16)
                    elif s[0] == "load_b":
                        n = s[1]
                        sync.wait_ge(b_stored, 16 * (j + 1))
                        sync.nop(nofuse=True)
                        wait(sync, u_ready, (j * N + n - ROWS + 1) * C)
                        sync.nop(nofuse=True)
                        sync.dma_start(b_ring[:, n % ROWS, :], b_dram[par, n:n + 1, :].to_broadcast([P, T])).then_inc(b_loaded[n % ROWS], 16)
                    elif s[0] == "store":
                        q = s[1]
                        sync.wait_ge(added, (r * Q + q + 1) * E)
                        sync.nop(nofuse=True)
                        sync.dma_start(out[bass.ds(r * T + q * P, P), :], x1[:, q, :]).then_inc(stored[q], 16)
                if isinstance(j, int) and j == -1:
                    sync.dma_start(w_exp[:], expert_w.rearrange("e (k p) n -> p e k n", p=P)).then_inc(experts_loaded, 16)

            run(sync, steps_of)
            for q in range(Q):
                sync.wait_ge(stored[q], 16 * BLOCKS)
                sync.nop(nofuse=True)

        @block.gpsimd
        def _(pool):
            nc.gpsimd.memset(ident[:], 0.0).then_inc(ident_zero, 1)
            pool.wait_ge(ident_zero, 1)
            nc.gpsimd.affine_select(out=ident[:], in_=ident[:], compare_op=ALU.not_equal, fill=1.0, base=0,
                                    pattern=[[-1, P]], channel_multiplier=1).then_inc(consts_ready, 1)
            nc.gpsimd.iota(lane[:], pattern=[[1, E]], base=0, channel_multiplier=0,
                           allow_small_or_imprecise_dtypes=True).then_inc(consts_ready, 1)
            nc.gpsimd.memset(minus_half[:], -0.5).then_inc(consts_ready, 1)
            nc.gpsimd.memset(minus_one[:], -1.0).then_inc(consts_ready, 1)
            pool.wait_ge(consts_ready, 4)
            pool.wait_ge(weights_loaded, 16 * WEIGHT_LOADS)

            def steps_of(j, par, steps):
                p, r = j + 1, j - 1
                for s in steps:
                    if s[0] == "norm_rstd":
                        q = s[1]
                        pool.wait_ge(stat_ready, p * Q + q + 1)
                        pool.nop(nofuse=True)
                        nc.gpsimd.tensor_scalar(veps[:, q:q + 1], mv[:, q, 1:2], LN_EPS, None, ALU.add).then_inc(veps_ready, 1)
                        pool.wait_ge(veps_ready, p * Q + q + 1)
                        nc.gpsimd.tensor_tensor(out=rstd[:, q:q + 1], in0=veps[:, q:q + 1], in1=minus_half[:], op=ALU.pow).then_inc(rstd_ready, 1)
                    elif s[0] == "u":
                        n, c = s[1], s[2]
                        if c == 0:
                            pool.wait_ge(b_loaded[n % ROWS], 16 * (j * (N // ROWS) + n // ROWS + 1))
                        if n == 0 and c == 0:
                            pool.wait_ge(xc_ready, (j + 1) * C)
                        g = n * C + c
                        wait(pool, scanned, j * N * C + g - UR + 1)
                        nc.gpsimd.tensor_tensor(out=u[:, g % UR, :], in0=xc[:, par, c, :], in1=b_ring[:, n % ROWS, :], op=ALU.mult).then_inc(u_ready, 1)
                        if n == N - 1:
                            if c == 0:
                                pool.wait_ge(ct_ready, (j + 1) * 2)
                            pool.wait_ge(u_ready, (j * N + n) * C + c + 1)
                            pool.nop(nofuse=True)
                            nc.gpsimd.tensor_scalar(xc[:, par, c, :], xc[:, par, c, :], d_skip[:, c:c + 1], None, ALU.mult).then_inc(skip_ready, 1)
                    elif s[0] == "y_gate":
                        q = s[1]
                        pool.wait_ge(y_skipped, r * Q + q + 1)
                        nc.gpsimd.tensor_tensor(out=y2[:, :, q * P:(q + 1) * P], in0=y2[:, :, q * P:(q + 1) * P],
                                                in1=sz[:, 1 - par, :, q * P:(q + 1) * P], op=ALU.mult).then_inc(y_gated, 1)
                    elif s[0] == "rstd2":
                        q = s[1]
                        pool.wait_ge(stat2_ready, r * Q + q + 1)
                        pool.nop(nofuse=True)
                        nc.gpsimd.tensor_scalar(veps2[:, q:q + 1], mv2[:, q, 1:2], LN_EPS, None, ALU.add).then_inc(veps2_ready, 1)
                        pool.wait_ge(veps2_ready, r * Q + q + 1)
                        nc.gpsimd.tensor_tensor(out=rstd2[:, q:q + 1], in0=veps2[:, q:q + 1], in1=minus_half[:], op=ALU.pow).then_inc(rstd2_ready, 1)
                    elif s[0] == "gate_weights":
                        q = s[1]
                        count = [0]

                        def link(ins):
                            count[0] += 1
                            ins.then_inc(weight_step, 1)
                            pool.wait_ge(weight_step, (r * Q + q) * WEIGHT_STEPS + count[0])
                            pool.nop(nofuse=True)

                        pool.wait_ge(top_ready, r * Q + q + 1)
                        pool.nop(nofuse=True)
                        link(nc.gpsimd.tensor_scalar(small[:, 0:1], top_prob[:, 0:1], top_prob[:, 1:2], EPS, ALU.add, ALU.add))
                        link(nc.gpsimd.tensor_tensor(out=small[:, 1:2], in0=small[:, 0:1], in1=minus_one[:, 0:1], op=ALU.pow))
                        link(nc.gpsimd.tensor_scalar(small[:, 2:4], top_prob[:, 0:2], small[:, 1:2], None, ALU.mult))
                        link(nc.gpsimd.tensor_tensor(out=small[:, 4:5], in0=small[:, 2:3], in1=small[:, 3:4], op=ALU.add))
                        link(nc.gpsimd.tensor_scalar(small[:, 5:6], small[:, 4:5], EPS, None, ALU.max))
                        link(nc.gpsimd.tensor_tensor(out=small[:, 5:6], in0=small[:, 5:6], in1=minus_one[:, 0:1], op=ALU.pow))
                        link(nc.gpsimd.tensor_scalar(small[:, 4:5], small[:, 4:5], EPS, 1.0, ALU.mult, ALU.add))
                        link(nc.gpsimd.tensor_scalar(small[:, 6:8], small[:, 2:4], small[:, 5:6], small[:, 4:5], ALU.mult, ALU.mult))
                        link(nc.gpsimd.tensor_scalar(pick[:, 0, :], lane[:], top_lane[:, 0:1], small[:, 6:7], ALU.is_equal, ALU.mult))
                        link(nc.gpsimd.tensor_scalar(pick[:, 1, :], lane[:], top_lane[:, 1:2], small[:, 7:8], ALU.is_equal, ALU.mult))
                        wait(pool, added, (r * Q + max(q - 1, 0)) * E)
                        nc.gpsimd.tensor_tensor(out=gate[:, q % 2, :], in0=pick[:, 0, :], in1=pick[:, 1, :], op=ALU.add).then_inc(gate_ready, 1)
                        assert count[0] == WEIGHT_STEPS

            run(pool, steps_of)

        @block.scalar
        def _(act):
            act.wait_ge(weights_loaded, 16 * WEIGHT_LOADS)
            nc.scalar.activation(neg_a[:], neg_a[:], ACT.Exp).then_inc(a_ready, 1)
            act.wait_ge(a_ready, 1)
            nc.scalar.activation(neg_a[:], neg_a[:], ACT.Copy, scale=-1.0).then_inc(a_ready, 1)
            act.wait_ge(a_ready, 2)

            def prep_wait(p, key):
                k = PREP_USE[key]
                act.wait_ge(prep_full[k % 2], p * (PREP_USES // 2) + k // 2 + 1)
                return prep_bank[k % 2], prep_free[k % 2]

            def post_wait(r, key):
                k = POST_USE[key]
                act.wait_ge(post_full[k % 2], r * (POST_USES // 2) + k // 2 + 1)
                return post_bank[k % 2], post_free[k % 2]

            def steps_of(j, par, steps):
                p, r = j + 1, j - 1
                for s in steps:
                    if s[0] == "decay":
                        n, c = s[1], s[2]
                        if n == 0 and c == 0:
                            act.wait_ge(dt_ready, j + 1)
                        g = n * C + c
                        wait(act, scanned, j * N * C + g - 1)
                        nc.scalar.activation(decay_bank[g % 2][:], dt[:, par, :], ACT.Exp, scale=neg_a[:, c, n:n + 1]).then_inc(decay_ready, 1)
                    elif s[0] == "norm_evict":
                        q = s[1]
                        ps, free = prep_wait(p, ("norm_T", q))
                        if not isinstance(j, int) or j > 0:
                            k = POST_USE["out_project", Q - 1]
                            act.wait_ge(post_full[k % 2], r * (POST_USES // 2) + k // 2 + 1)
                        nc.scalar.activation(xnT[:, :, q * P:(q + 1) * P], ps[:].rearrange("p (k t) -> p k t", k=C), ACT.Copy).then_inc(free, 1)
                        act.wait_ge(free, p * (PREP_USES // 2) + PREP_USE["norm_T", q] // 2 + 1)
                        act.sem_inc(xnT_ready, 1)
                    elif s[0] == "project_evict":
                        m = s[1]
                        ps, free = prep_wait(p, ("project", m))
                        k = PREP_USE["project", m]
                        if m < C:
                            wait(act, conv_tap, p * C * TAPS)
                            act.wait_ge(edge_ready, p + 1)
                            nc.scalar.activation(xs[:, m, TAPS - 1:], ps[:], ACT.Copy).then_inc(free, 1)
                            act.wait_ge(free, p * (PREP_USES // 2) + k // 2 + 1)
                            act.sem_inc(xs_ready, 1)
                        else:
                            wait(act, y_gated, (p - 1) * Q)
                            nc.scalar.activation(sz[:, 1 - par, m - C, :], ps[:], ACT.Copy).then_inc(free, 1)
                            act.wait_ge(free, p * (PREP_USES // 2) + k // 2 + 1)
                    elif s[0] == "silu":
                        for c in range(C):
                            act.wait_ge(conv_tap, (p * C + c + 1) * TAPS)
                            nc.scalar.activation(xc[:, 1 - par, c, :], xc[:, 1 - par, c, :], ACT.Silu, bias=b_conv[:, c:c + 1]).then_inc(xc_ready, 1)
                        nc.scalar.activation(sz[:, 1 - par], sz[:, 1 - par], ACT.Silu).then_inc(sz_ready, 1)
                    elif s[0] == "dt_exp":
                        ps, _ = prep_wait(p, ("dt_project", 0))
                        nc.scalar.activation(sp[:], ps[:], ACT.Abs).then_inc(sp_step, 1)
                        act.wait_ge(sp_step, p * 3 + 1)
                        nc.scalar.activation(sp[:], sp[:], ACT.Exp, scale=-1.0).then_inc(sp_step, 1)
                        act.wait_ge(sp_step, p * 3 + 2)
                        nc.scalar.activation(sp[:], sp[:], ACT.Ln, bias=1.0).then_inc(sp_step, 1)
                    elif s[0] == "c_evict":
                        i = s[1]
                        ps, free = prep_wait(p, ("c_project", i))
                        wait(act, summed, (p - 1) * N * Q)
                        nc.scalar.activation(ct[:, 1 - par, 2 * i:2 * i + 2, :], ps[:, 0:2 * N].rearrange("p (q n) -> p q n", q=2), ACT.Copy).then_inc(ct_ready, 1)
                        act.wait_ge(ct_ready, p * 2 + i + 1)
                        act.sem_inc(free, 1)
                    elif s[0] == "norm2_evict":
                        q = s[1]
                        ps, free = post_wait(r, ("norm2_T", q))
                        k = POST_USE["norm2_T", q]
                        if q >= 2:
                            last = POST_USE["expert", (q - 1) * E - 1]
                            act.wait_ge(post_full[last % 2], r * (POST_USES // 2) + last // 2 + 1)
                        nc.scalar.activation(xn2T[:, q % 2], ps[:].rearrange("p (k t) -> p k t", k=C), ACT.Copy).then_inc(xn2T_ready, 1)
                        act.wait_ge(xn2T_ready, r * Q + q + 1)
                        act.sem_inc(free, 1)
                    elif s[0] == "gate_exp":
                        q = s[1]
                        act.wait_ge(logits_ready, r * Q + q + 1)
                        nc.scalar.activation(prob[:], logit[:], ACT.Exp, bias=neg_top[:], accum_out=prob_sum[:]).then_inc(prob_ready, 1)

            run(act, steps_of)

        @block.vector
        def _(dve):
            dve.wait_ge(weights_loaded, 16 * WEIGHT_LOADS)
            nc.vector.tensor_copy(w_dt[:], w_xp[:, :, 2 * N:2 * N + 1].to_broadcast([P, C, P])).then_inc(consts_ready, 1)

            def prep_wait(p, key):
                k = PREP_USE[key]
                dve.wait_ge(prep_full[k % 2], p * (PREP_USES // 2) + k // 2 + 1)
                return prep_bank[k % 2], prep_free[k % 2]

            def post_wait(r, key):
                k = POST_USE[key]
                dve.wait_ge(post_full[k % 2], r * (POST_USES // 2) + k // 2 + 1)
                return post_bank[k % 2], post_free[k % 2]

            def steps_of(j, par, steps):
                p, r = j + 1, j - 1
                for s in steps:
                    if s[0] == "scan":
                        n, c = s[1], s[2]
                        g = n * C + c
                        dve.wait_ge(decay_ready, j * N * C + g + 1)
                        dve.wait_ge(u_ready, j * N * C + g + 1)
                        wait(dve, hT_ready, (j * N + n - 1) * Q)
                        first = 0.0
                        if par == 1:
                            dve.wait_ge(h_kept, (j - 1) * (N // 2) + n + 1)
                            first = h_last[:, n, c:c + 1]
                        nc.vector.tensor_tensor_scan(out=h[:, n % 2, c, :], data0=decay_bank[g % 2][:], data1=u[:, g % UR, :],
                                                     initial=first, op0=ALU.mult, op1=ALU.add).then_inc(scanned, 1)
                    elif s[0] == "keep_h" and par == 0:
                        n = s[1]
                        dve.wait_ge(scanned, (j * N + n + 1) * C)
                        nc.vector.tensor_copy(h_last[:, n, :], h[:, n % 2, :, T - 1]).then_inc(h_kept, 1)
                    elif s[0] == "h_sum":
                        m, q, blk = s[1], s[2], s[3]
                        i, ip = j + blk, par if blk == 0 else 1 - par
                        dve.wait_ge(hT_ready, (i * N + m) * Q + q + 1)
                        if m == 0:
                            dve.wait_ge(ct_ready, (i + 1) * 2)
                            yk = POST_USE["y_T", q]
                            wait(dve, post_full[yk % 2], (i - 1) * (POST_USES // 2) + yk // 2 + 1)
                            nc.vector.tensor_scalar(acc[:, q, :], hT_bank[q % 2][:], ct[:, ip, q, m:m + 1], None, ALU.mult).then_inc(summed, 1)
                        else:
                            dve.wait_ge(summed, (i * N + m - 1) * Q + q + 1)
                            nc.vector.scalar_tensor_tensor(out=acc[:, q, :], in0=hT_bank[q % 2][:], scalar=ct[:, ip, q, m:m + 1],
                                                           in1=acc[:, q, :], op0=ALU.mult, op1=ALU.add).then_inc(summed, 1)
                    elif s[0] == "norm_stat":
                        q = s[1]
                        dve.wait_ge(x_loaded[q % 2], 16 * (2 * p + q // 2 + 1))
                        nc.vector.bn_stats(out=stat[:, q, :], in_=xn[:, q % 2, :]).then_inc(stat_half, 1)
                        dve.wait_ge(stat_half, p * Q + q + 1)
                        dve.nop(nofuse=True)
                        nc.vector.bn_aggr(out=mv[:, q, :], in_=stat[:, q, :]).then_inc(stat_ready, 1)
                    elif s[0] == "norm_apply":
                        q = s[1]
                        dve.wait_ge(rstd_ready, p * Q + q + 1)
                        nc.vector.tensor_scalar(xn[:, q % 2, :], xn[:, q % 2, :], mv[:, q, 0:1], rstd[:, q:q + 1],
                                                ALU.subtract, ALU.mult).then_inc(xn_ready, 1)
                    elif s[0] == "conv_edge":
                        wait(dve, conv_tap, p * C * TAPS)
                        if par == 1:
                            nc.vector.memset(xs[:, :, 0:TAPS - 1], 0.0).then_inc(edge_ready, 1)
                        else:
                            nc.vector.tensor_copy(xs[:, :, 0:TAPS - 1], xs[:, :, T:T + TAPS - 1]).then_inc(edge_ready, 1)
                    elif s[0] == "conv":
                        c = s[1]
                        dve.wait_ge(xs_ready, p * C + c + 1)
                        dst = xc[:, 1 - par, c, :]
                        nc.vector.tensor_scalar(dst, xs[:, c, 0:T], w_conv[:, c, 0:1], None, ALU.mult).then_inc(conv_tap, 1)
                        for k in range(1, TAPS):
                            dve.wait_ge(conv_tap, (p * C + c) * TAPS + k)
                            nc.vector.scalar_tensor_tensor(out=dst, in0=xs[:, c, k:k + T], scalar=w_conv[:, c, k:k + 1], in1=dst,
                                                           op0=ALU.mult, op1=ALU.add).then_inc(conv_tap, 1)
                    elif s[0] == "dt_plus":
                        dve.wait_ge(sp_step, (p + 1) * 3)
                        k = PREP_USE["dt_project", 0]
                        ps, free = prep_bank[k % 2], prep_free[k % 2]
                        wait(dve, decay_ready, (p - 1) * N * C)
                        nc.vector.scalar_tensor_tensor(out=dt[:, 1 - par, :], in0=ps[:], scalar=0.0, in1=sp[:],
                                                       op0=ALU.max, op1=ALU.add).then_inc(dt_ready, 1)
                        dve.wait_ge(dt_ready, p + 1)
                        dve.sem_inc(free, 1)
                    elif s[0] == "b_scale":
                        ps, free = prep_wait(p, ("b_project", 0))
                        dve.wait_ge(dt_ready, p + 1)
                        wait(dve, b_stored, 16 * p)
                        nc.vector.tensor_tensor(out=b_rows[:], in0=ps[0:N, :], in1=dt[0:N, 1 - par, :], op=ALU.mult).then_inc(b_rows_ready, 1)
                        dve.wait_ge(b_rows_ready, p + 1)
                        dve.sem_inc(free, 1)
                    elif s[0] == "y_skip":
                        q = s[1]
                        ps, free = post_wait(r, ("y_T", q))
                        k = POST_USE["y_T", q]
                        if q == 0:
                            dve.wait_ge(skip_ready, (r + 1) * C)
                            if not isinstance(j, int) or j < BLOCKS:
                                k = PREP_USE["project", M - 1]
                                dve.wait_ge(prep_full[k % 2], j * (PREP_USES // 2) + k // 2 + 1)
                            last = POST_USE["out_project", Q - 1]
                            wait(dve, post_full[last % 2], r * (POST_USES // 2))
                        nc.vector.tensor_tensor(out=y2[:, :, q * P:(q + 1) * P], in0=ps[:].rearrange("p (k t) -> p k t", k=C),
                                                in1=xc[:, 1 - par, :, q * P:(q + 1) * P], op=ALU.add).then_inc(y_skipped, 1)
                        dve.wait_ge(y_skipped, r * Q + q + 1)
                        dve.sem_inc(free, 1)
                    elif s[0] == "residual":
                        q = s[1]
                        ps, free = post_wait(r, ("out_project", q))
                        dve.wait_ge(res_loaded[q], 16 * (r + 1))
                        nc.vector.tensor_tensor(out=x1[:, q, :], in0=ps[:], in1=x1[:, q, :], op=ALU.add).then_inc(x1_ready, 1)
                        dve.wait_ge(x1_ready, r * Q + q + 1)
                        dve.sem_inc(free, 1)
                        nc.vector.bn_stats(out=stat2[:, q, :], in_=x1[:, q, :]).then_inc(stat2_half, 1)
                        dve.wait_ge(stat2_half, r * Q + q + 1)
                        dve.nop(nofuse=True)
                        nc.vector.bn_aggr(out=mv2[:, q, :], in_=stat2[:, q, :]).then_inc(stat2_ready, 1)
                    elif s[0] == "norm2":
                        q = s[1]
                        dve.wait_ge(rstd2_ready, r * Q + q + 1)
                        dve.wait_ge(stat2_ready, r * Q + q + 1)
                        if q:
                            last = POST_USE["norm2_T", q - 1]
                            dve.wait_ge(post_full[last % 2], r * (POST_USES // 2) + last // 2 + 1)
                        nc.vector.tensor_scalar(xn2[:], x1[:, q, :], mv2[:, q, 0:1], rstd2[:, q:q + 1], ALU.subtract, ALU.mult).then_inc(xn2_ready, 1)
                    elif s[0] == "gate_logits":
                        q = s[1]
                        ps, free = post_wait(r, ("router", q))
                        base = (r * Q + q) * GATE_STEPS
                        nc.vector.tensor_tensor(out=logit[:], in0=ps[:, 0:E], in1=b_router[:], op=ALU.add).then_inc(gate_step, 1)
                        dve.wait_ge(gate_step, base + 1)
                        dve.sem_inc(free, 1)
                        nc.vector.max(top_logit[:], logit[:]).then_inc(gate_step, 1)
                        dve.wait_ge(gate_step, base + 2)
                        nc.vector.tensor_scalar(neg_top[:], top_logit[:, 0:1], -1.0, None, ALU.mult).then_inc(logits_ready, 1)
                    elif s[0] == "gate_top":
                        q = s[1]
                        base = (r * Q + q) * GATE_STEPS
                        dve.wait_ge(prob_ready, r * Q + q + 1)
                        nc.vector.reciprocal(neg_top[:], prob_sum[:]).then_inc(gate_step, 1)
                        dve.wait_ge(gate_step, base + 3)
                        nc.vector.tensor_scalar(prob[:], prob[:], neg_top[:], None, ALU.mult).then_inc(gate_step, 1)
                        dve.wait_ge(gate_step, base + 4)
                        wait(dve, gate_ready, r * Q + q)
                        dve.nop(nofuse=True)
                        nc.vector.max(top_prob[:], prob[:]).then_inc(gate_step, 1)
                        dve.wait_ge(gate_step, base + 5)
                        dve.nop(nofuse=True)
                        nc.vector.max_index(top_at[:], top_prob[:], prob[:]).then_inc(gate_step, 1)
                        dve.wait_ge(gate_step, base + 6)
                        nc.vector.tensor_copy(top_lane[:], top_at[:, 0:2]).then_inc(gate_step, 1)
                        dve.wait_ge(gate_step, base + 7)
                        dve.sem_inc(top_ready, 1)
                    elif s[0] == "expert_add":
                        q, e = units[s[1]]
                        ps, free = post_wait(r, ("expert", s[1]))
                        if e == 0:
                            dve.wait_ge(gate_ready, r * Q + q + 1)
                        wait(dve, added, r * Q * E + s[1])
                        nc.vector.scalar_tensor_tensor(out=x1[:, q, :], in0=ps[:], scalar=gate[:, q % 2, e:e + 1], in1=x1[:, q, :],
                                                       op0=ALU.mult, op1=ALU.add).then_inc(added, 1)
                        dve.wait_ge(added, r * Q * E + s[1] + 1)
                        dve.sem_inc(free, 1)

            run(dve, steps_of)

        @block.tensor
        def _(pe):
            pe.wait_ge(consts_ready, 5)
            pe.wait_ge(weights_loaded, 16 * WEIGHT_LOADS)

            def prep_use(p, key):
                k = PREP_USE[key]
                wait(pe, prep_free[k % 2], p * (PREP_USES // 2) + k // 2)
                return prep_bank[k % 2], prep_full[k % 2]

            def post_use(r, key):
                k = POST_USE[key]
                wait(pe, post_free[k % 2], r * (POST_USES // 2) + k // 2)
                return post_bank[k % 2], post_full[k % 2]

            def product(ps, left, right):
                for k in range(C):
                    last = nc.tensor.matmul(ps, left(k), right(k), start=(k == 0), stop=(k == C - 1))
                return last

            def transposes(ps, tile):
                for k in range(C):
                    last = nc.tensor.transpose(ps[:, k * P:(k + 1) * P], tile(k), ident[:])
                return last

            def steps_of(j, par, steps):
                p, r = j + 1, j - 1
                for s in steps:
                    if s[0] == "h_T":
                        m, q, blk = s[1], s[2], s[3]
                        i = j + blk
                        pe.wait_ge(scanned, (i * N + m + 1) * C)
                        wait(pe, summed, (i * N + m) * Q + q - 1)
                        transposes(hT_bank[q % 2], lambda k: h[:, m % 2, k, q * P:(q + 1) * P]).then_inc(hT_ready, 1)
                    elif s[0] == "norm_T":
                        q = s[1]
                        ps, full = prep_use(p, s)
                        pe.wait_ge(xn_ready, p * Q + q + 1)
                        transposes(ps, lambda k: xn[:, q % 2, k * P:(k + 1) * P]).then_inc(full, 1)
                    elif s[0] == "project":
                        m = s[1]
                        ps, full = prep_use(p, s)
                        if m == 0:
                            pe.wait_ge(xnT_ready, (p + 1) * Q)
                        product(ps[:], lambda k: w_in[:, k, m * P:(m + 1) * P], lambda k: xnT[:, k, :]).then_inc(full, 1)
                    elif s[0] == "dt_project":
                        ps, full = prep_use(p, s)
                        pe.wait_ge(xc_ready, (p + 1) * C)
                        product(ps[:], lambda k: w_dt[:, k, :], lambda k: xc[:, 1 - par, k, :]).then_inc(full, 1)
                    elif s[0] == "b_project":
                        ps, full = prep_use(p, s)
                        product(ps[0:N, :], lambda k: w_xp[:, k, 0:N], lambda k: xc[:, 1 - par, k, :]).then_inc(full, 1)
                    elif s[0] == "c_project":
                        ps, full = prep_use(p, s)
                        for i in range(2):
                            q = 2 * s[1] + i
                            last = product(ps[:, i * N:(i + 1) * N], lambda k: xc[:, 1 - par, k, q * P:(q + 1) * P],
                                           lambda k: w_xp[:, k, N:2 * N])
                        last.then_inc(full, 1)
                    elif s[0] == "y_T":
                        q = s[1]
                        ps, full = post_use(r, s)
                        pe.wait_ge(summed, (r * N + N - 1) * Q + q + 1)
                        transposes(ps, lambda k: acc[:, q, k * P:(k + 1) * P]).then_inc(full, 1)
                    elif s[0] == "out_project":
                        q = s[1]
                        ps, full = post_use(r, s)
                        pe.wait_ge(y_gated, r * Q + q + 1)
                        product(ps[:], lambda k: y2[:, k, q * P:(q + 1) * P], lambda k: w_out[:, k, :]).then_inc(full, 1)
                    elif s[0] == "norm2_T":
                        q = s[1]
                        ps, full = post_use(r, s)
                        pe.wait_ge(xn2_ready, r * Q + q + 1)
                        transposes(ps, lambda k: xn2[:, k * P:(k + 1) * P]).then_inc(full, 1)
                    elif s[0] == "router":
                        q = s[1]
                        ps, full = post_use(r, s)
                        pe.wait_ge(xn2T_ready, r * Q + q + 1)
                        product(ps[:, 0:E], lambda k: xn2T[:, q % 2, k, :], lambda k: w_router[:, k, :]).then_inc(full, 1)
                    elif s[0] == "expert":
                        q, e = units[s[1]]
                        if s[1] == 0 and isinstance(j, int):
                            pe.wait_ge(experts_loaded, 16)
                        ps, full = post_use(r, s)
                        product(ps[:], lambda k: xn2T[:, q % 2, k, :], lambda k: w_exp[:, e, k, :]).then_inc(full, 1)

            run(pe, steps_of)


_INS = ['x', 'in_w', 'conv_w', 'conv_b', 'xp_w', 'a_log', 'd_param', 'out_w', 'router_w', 'router_b', 'expert_w']


def kernel(**inputs):
    import numpy as _np
    import concourse.bacc as _bacc
    from concourse import mybir as _mybir
    from concourse.bass_utils import run_bass_kernel_spmd as _run

    a = {k: _np.asarray(v) for k, v in inputs.items()}
    shape = a['L0_attn_x'].shape
    given = {
        'x': a['L0_attn_x'].reshape(-1, shape[-1]),
        'in_w': a['L0_attn_in_proj_w'].T,
        'conv_w': a['L0_attn_conv_w'],
        'conv_b': a['L0_attn_conv_b'].reshape(-1, 128).T,
        'xp_w': a['L0_attn_x_proj_w'].T,
        'a_log': a['L0_attn_A_log'],
        'd_param': a['L0_attn_D_param'].reshape(-1, 128).T,
        'out_w': a['L0_attn_out_proj_w'].T,
        'router_w': a['L0_ffn_router_w'].T,
        'router_b': a['L0_ffn_router_b'],
        'expert_w': a['L0_ffn_expert_weights'],
    }
    nc = _bacc.Bacc("TRN2", target_bir_lowering=False, num_devices=1)
    arrays, args = {}, []
    for name in _INS:
        v = _np.ascontiguousarray(given[name])
        arrays[f"in_{name}"] = v
        args.append(nc.dram_tensor(f"in_{name}", v.shape, _mybir.dt.from_np(v.dtype), kind="ExternalInput").ap())
    out = nc.dram_tensor("out", given['x'].shape, _mybir.dt.from_np(given['x'].dtype), kind="ExternalOutput").ap()
    mamba_moe_kernel(nc, *args, out)
    r = _run(nc, [arrays], core_ids=[0])
    return r.results[0]["out"].reshape(shape)
```

```python
import concourse.bass as bass
from concourse import mybir
from contextlib import ExitStack



def mamba_moe_kernel(nc, x, in_w, conv_w, conv_b, xp_w, a_log, d_param, out_w,
                     router_w, router_b, expert_w, out):
    fp32 = mybir.dt.float32
    u32 = mybir.dt.uint32
    i32 = mybir.dt.int32
    AX = mybir.AxisListType
    ALU = mybir.AluOpType
    ACT = mybir.ActivationFunctionType

    P = 128
    TOKENS, D = x.shape
    SEQ = 1024
    T = 512
    Q = T // P
    C = D // P
    N = a_log.shape[1]
    TAPS = conv_w.shape[1]
    E = expert_w.shape[0]
    BLOCKS = TOKENS // T
    BATCHES = TOKENS // SEQ
    LN_EPS = 1e-5
    EPS = 1e-10
    ROWS = 2
    UR = 4
    M = 2 * C
    TOP = 2
    SQ = SEQ // P
    CAP = SEQ
    XT = TOP * SQ + E
    HALF_XT = XT // 2
    REGION = E * CAP
    RESULTS = XT * P

    prep, post, experts, comb = [], [], [], []
    for q in range(Q):
        at = [18, 20, 28, 30][q]
        prep += [([8, 9, 19, 21][q], ("load_x", q)), (at - 6, ("norm_stat", q)), (at - 2, ("norm_rstd", q)),
                 (at - 1, ("norm_apply", q)), (at, ("norm_T", q)), (at + 2, ("norm_evict", q))]
    prep += [(29, ("conv_edge", 0))]
    for m in range(M):
        at = 32 + 2 * m
        prep += [(at, ("project", m)), (at + 3, ("project_evict", m))]
        if m < C:
            prep += [(at + 4, ("conv", m))]
    prep += [(49, ("silu", 0)), (50, ("dt_project", 0)), (53, ("b_project", 0)), (52, ("dt_exp", 0)), (54, ("dt_plus", 0)),
             (55, ("b_scale", 0)), (56, ("b_store", 0)), (54, ("c_project", 0)), (55, ("c_project", 1)),
             (56, ("c_evict", 0)), (57, ("c_evict", 1))]

    for q in range(Q):
        at = [5, 7, 12, 16][q]
        post += [(q, ("y_T", q)), (q + 1, ("y_skip", q)), (q + 4, ("y_gate", q)), ([0, 0, 12, 14][q], ("load_res", q)),
                 (at, ("out_project", q)), (at + 2 + (q < 2), ("residual", q)), (at + 7, ("rstd2", q)), (at + 4, ("store_x1", q))]
        at = [10, 15, 36, 41][q]
        post += [(at, ("load_x1", q)), (at + 3, ("norm2", q)), (at + 4, ("norm2_T", q)), (at + 6, ("norm2_evict", q)),
                 (at + 7, ("router", q)), (at + 8, ("gate_logits", q)), (at + 10, ("gate_exp", q)), (at + 11, ("gate_top", q)),
                 (at + 15, ("gate_weights", q)), (at + 17, ("rank", q)), (at + 18, ("row_of", q)), (at + 22, ("scatter", q))]

    experts += [(9, ("rows_load", 0)), (12, ("rows_T", 0)), (12, ("rows_load", 1)), (14, ("rows_evict", 0))]
    for i, at in enumerate([15, 18, 21, 24, 27, 30, 48, 54, 56, 58, 60, 62]):
        if i + 1 < HALF_XT:
            experts += [(at, ("rows_T", i + 1)), (at + 1, ("rows_evict", i + 1))]
        if i + 2 < HALF_XT:
            experts += [(at, ("rows_load", i + 2))]
        experts += [(at, ("expert", i)), (min(at + 2, N * C - 1), ("expert_evict", i)), (min(at + 3, N * C - 1), ("rows_store", i))]

    for q in range(Q):
        at = [10, 23, 36, 49][q]
        comb += [(at, ("fetch", q)), (at, ("gather", q, 0)), (at + 3, ("add_row", q, 0)), (at + 7, ("gather", q, 1)),
                 (at + 9, ("add_row", q, 1)), (at + 10, ("store", q))]

    def iteration(j, half):
        def on(first, last):
            return not isinstance(j, int) or first <= j <= last
        scan, tail = on(0, BLOCKS - 1), on(1, BLOCKS)
        do_prep, do_post = on(-1, BLOCKS - 2), on(1, BLOCKS)
        side = sum([x for x, do in ((comb, on(5, BLOCKS + 4)), (post, do_post), (prep, do_prep),
                                    (experts, on(3, BLOCKS + 2))) if do], [])
        if half == 1:
            side = [(6, ("slots_age", 0))] * on(3, BLOCKS + 3) + [(6, ("new_sequence", 0))] * on(1, BLOCKS + 1) + side
        place = {at: [s for a, s in side if a == at] for at in range(N * C)}
        assert sum(len(x) for x in place.values()) == len(side)
        steps = []
        for n in range(N):
            m, blk = (N - 1, -1) if n == 0 else (n - 1, 0)
            summing = tail if n == 0 else scan
            if summing:
                steps += [("h_T", m, 0, blk), ("h_T", m, 1, blk)]
            if scan and n + 1 < N:
                steps.append(("load_b", n + 1, 0))
            elif do_prep and n + 1 == N:
                steps.append(("load_b", 0, 1))
            for c in range(C):
                if scan:
                    steps += [("decay", n, c), ("u", n, c), ("scan", n, c)]
                if summing:
                    steps.append(("h_sum", m, c, blk))
                    if c + 2 < Q:
                        steps.append(("h_T", m, c + 2, blk))
                steps += place[n * C + c]
            if scan:
                steps.append(("keep_h", n))
        return steps

    WORK = 4
    TAKES = {"norm_T": "norm_evict", "project": "project_evict", "dt_project": "dt_plus", "b_project": "b_scale",
             "c_project": "c_evict", "y_T": "y_skip", "out_project": "residual", "norm2_T": "norm2_evict",
             "router": "gate_logits", "rank": "row_of", "rows_T": "rows_evict", "expert": "expert_evict"}
    LOOP_FROM = 7

    def takes(j):
        out, freed = [], set()
        for s in iteration(j, j % 2):
            if s[0] in TAKES:
                if len(out) >= WORK:
                    old = out[-WORK]
                    assert (TAKES[old[0]], old[1]) in freed, (s, old)
                out.append(s)
            freed.add(s[:2])
        return {s: k for k, s in enumerate(out)}

    ORDINAL = {j: takes(j) for j in range(-1, max(BLOCKS + 5, LOOP_FROM + 2))}
    FIRST_USE = {j: sum(len(ORDINAL[i]) for i in range(-1, j)) for j in ORDINAL}
    LOOP_USES = len(ORDINAL[LOOP_FROM]) if BLOCKS > LOOP_FROM + 1 else WORK
    assert LOOP_USES % WORK == 0

    def use_of(j, half, key):
        if isinstance(j, int):
            k = FIRST_USE[j] + ORDINAL[j][key]
            return k % WORK, k // WORK
        at = LOOP_FROM if half == 1 else LOOP_FROM + 1
        k = FIRST_USE[at] + ORDINAL[at][key]
        return k % WORK, (j - at) * (LOOP_USES // WORK) + k // WORK

    ctx = ExitStack()
    with ctx:
        def sb(name, shape, dt=fp32):
            return ctx.enter_context(nc.sbuf_tensor(name, shape, dt))

        def sem(name):
            return ctx.enter_context(nc.semaphore(name))

        w_in = sb("w_in", [P, C, 2 * D])
        w_out = sb("w_out", [P, C, D])
        w_exp = sb("w_exp", [P, E, C * D])
        w_xp = sb("w_xp", [P, C, 2 * N + 1])
        w_router = sb("w_router", [P, C, E])
        b_router = sb("b_router", [P, E])
        w_conv = sb("w_conv", [P, C, TAPS])
        b_conv = sb("b_conv", [P, C])
        d_skip = sb("d_skip", [P, C])
        neg_a = sb("neg_a", [P, C, N])
        ident = sb("ident", [P, P])
        earlier = sb("earlier", [P, P])
        ones = sb("ones", [P, E])
        lane = sb("lane", [P, E])
        tile_no = sb("tile_no", [1, XT])
        minus_half = sb("minus_half", [P, 1])
        minus_one = sb("minus_one", [P, 2])
        xn = sb("xn", [P, 2, D])
        stat = sb("stat", [P, Q, 6])
        mv = sb("mv", [P, Q, 2])
        veps = sb("veps", [P, Q])
        rstd = sb("rstd", [P, Q])
        xs = sb("xs", [P, C, TAPS - 1 + T])
        sp = xs[:, 0:2, TAPS - 1:TAPS - 1 + T // 2]
        b_rows = xs[0:N, 2:4, TAPS - 1:TAPS - 1 + T // 2]
        xc = sb("xc", [P, 2, C, T])
        sz = sb("sz", [P, 2, C, T])
        dt = sb("dt", [P, 2, T])
        ct = sb("ct", [P, 2, Q, N])
        b_ring = sb("b_ring", [P, ROWS, T])
        u = sb("u", [P, UR, T])
        h = sb("h", [P, 2, C, T])
        h_last = sb("h_last", [P, N, C])
        acc = sb("acc", [P, Q, D])
        y2 = sb("y2", [P, C, T])
        xnT = y2
        x1 = sb("x1", [P, 2, D])
        stat2 = sb("stat2", [P, Q, 6])
        mv2 = sb("mv2", [P, Q, 2])
        veps2 = sb("veps2", [P, Q])
        rstd2 = sb("rstd2", [P, Q])
        xn2 = sb("xn2", [P, 2, D])
        xn2T = sb("xn2T", [P, C, P])
        logit = sb("logit", [P, E])
        top_logit = sb("top_logit", [P, 8])
        neg_top = sb("neg_top", [P, 1])
        prob = sb("prob", [P, E])
        prob_sum = sb("prob_sum", [P, 1])
        top_prob = sb("top_prob", [P, 8])
        top_at = sb("top_at", [P, 8], u32)
        top_lane = sb("top_lane", [P, TOP])
        small = sb("small", [P, 8])
        pick = sb("pick", [P, SQ, TOP, E])
        mask = sb("mask", [P, E])
        mask_sum = sb("mask_sum", [P, E])
        row_base = sb("row_base", [P, E + 1])
        row_flip = sb("row_flip", [P, E + 1])
        rank_row = sb("rank_row", [P, E])
        picked_row = sb("picked_row", [P, TOP, E])
        row_f32 = sb("row_f32", [P, SQ, TOP])
        row_at = sb("row_at", [P, SQ, TOP], u32)
        rows_of = [sb(f"rows_of{i}", [P, SQ, TOP], u32) for i in range(2)]
        weight_of = [sb(f"weight_of{i}", [P, SQ, TOP]) for i in range(3)]
        fill = sb("fill", [P, E], i32)
        tiles_i = sb("tiles_i", [P, E], i32)
        tiles_f = sb("tiles_f", [P, E])
        tiles_to = sb("tiles_to", [P, E])
        shift = sb("shift", [P, E])
        result_f = sb("result_f", [P, SQ, TOP])
        expert_f = sb("expert_f", [1, XT])
        before_f = sb("before_f", [1, XT])
        row_f = sb("row_f", [1, XT])
        tile_row = sb("tile_row", [1, XT], i32)
        tile_expert = sb("tile_expert", [1, XT], i32)
        xe = sb("xe", [P, D])
        xeT = sb("xeT", [P, 2, C, P])
        ye = sb("ye", [P, D])
        x_out = sb("x_out", [P, D])
        y_row = sb("y_row", [P, D])
        token_shift = y_row[:, 0:SQ * TOP * E].rearrange("p (t k e) -> p t k e", t=SQ, k=TOP)
        past = y_row[0:1, SQ * TOP * E:SQ * TOP * E + XT * E].rearrange("p (i e) -> p i e", i=XT)

        def bank(name):
            return ctx.enter_context(nc.psum_tensor(name, [P, 512], fp32))

        decay_bank = [bank(f"decay{i}") for i in range(2)]
        hT_bank = [bank(f"hT{i}") for i in range(2)]
        work_bank = [bank(f"work{i}") for i in range(WORK)]

        b_dram = nc.dram_tensor("b_scratch", [2, N, T], fp32, kind="Internal").ap()
        x1_dram = nc.dram_tensor("x1_scratch", [TOKENS, D], fp32, kind="Internal").ap()
        row_dram = nc.dram_tensor("row_scratch", [2 * REGION, D], fp32, kind="Internal").ap()
        res_dram = nc.dram_tensor("result_scratch", [2 * RESULTS, D], fp32, kind="Internal").ap()

        work_full = [sem(f"work_full{i}") for i in range(WORK)]
        work_free = [sem(f"work_free{i}") for i in range(WORK)]
        weights_loaded = sem("weights_loaded")
        experts_loaded = sem("experts_loaded")
        const_step = sem("const_step")
        rows_zeroed = sem("rows_zeroed")
        zeros_ready = sem("zeros_ready")
        a_ready = sem("a_ready")
        x_loaded = [sem(f"x_loaded{i}") for i in range(2)]
        stat_half = sem("stat_half")
        stat_ready = sem("stat_ready")
        veps_ready = sem("veps_ready")
        rstd_ready = sem("rstd_ready")
        xn_ready = sem("xn_ready")
        edge_ready = sem("edge_ready")
        conv_tap = sem("conv_tap")
        xc_ready = sem("xc_ready")
        sz_ready = sem("sz_ready")
        sp_step = sem("sp_step")
        b_stored = sem("b_stored")
        b_loaded = [sem(f"b_loaded{i}") for i in range(ROWS)]
        skip_ready = sem("skip_ready")
        u_ready = sem("u_ready")
        decay_ready = sem("decay_ready")
        scanned = sem("scanned")
        h_kept = sem("h_kept")
        hT_ready = sem("hT_ready")
        summed = sem("summed")
        y_gated = sem("y_gated")
        res_loaded = [sem(f"res_loaded{i}") for i in range(2)]
        x1_loaded = [sem(f"x1_loaded{i}") for i in range(2)]
        x1_stored = [sem(f"x1_stored{i}") for i in range(2)]
        stat2_half = sem("stat2_half")
        stat2_ready = sem("stat2_ready")
        veps2_ready = sem("veps2_ready")
        rstd2_ready = sem("rstd2_ready")
        xn2_ready = sem("xn2_ready")
        gate_step = sem("gate_step")
        logits_ready = sem("logits_ready")
        prob_ready = sem("prob_ready")
        top_ready = sem("top_ready")
        mask_summed = sem("mask_summed")
        weight_step = sem("weight_step")
        mask_ready = sem("mask_ready")
        fill_ready = sem("fill_ready")
        row_step = sem("row_step")
        row_summed = sem("row_summed")
        rows_ready = sem("rows_ready")
        scattered = [sem(f"scattered{i}") for i in range(2)]
        aged = sem("aged")
        flipped = sem("flipped")
        table_step = sem("table_step")
        rows_loaded = sem("rows_loaded")
        rows_stored = sem("rows_stored")
        gathered = sem("gathered")
        x_out_loaded = sem("x_out_loaded")
        row_added = sem("row_added")
        stored = sem("stored")

        GATE_STEPS, WEIGHT_STEPS, TABLE_STEPS, AGE_STEPS = 5, 9, 19, 3
        WEIGHT_LOADS = 9
        ZERO_LOADS = 9

        def wait(eng, s, value):
            if not isinstance(value, int) or value > 0:
                eng.wait_ge(s, value)

        def hold(eng, s, value):
            wait(eng, s, value)
            eng.nop(nofuse=True)

        def wait_full(eng, j, half, key):
            bank_no, before = use_of(j, half, key)
            eng.wait_ge(work_full[bank_no], before + 1)
            return work_bank[bank_no], work_free[bank_no]

        def wait_product(eng, j, half, key, ps=None):
            bank_no, before = use_of(j, half, key)
            if work_bank[bank_no] is not ps:
                eng.wait_ge(work_full[bank_no], before + 1)

        def wait_used(eng, j, half, key, ps=None):
            bank_no, before = use_of(j, half, key)
            if work_bank[bank_no] is not ps:
                eng.wait_ge(work_free[bank_no], before + 1)

        def run(eng, steps_of):
            looped = max(BLOCKS - LOOP_FROM - 1, 0) // 2
            for j in range(-1, LOOP_FROM):
                steps_of(j, j % 2, j // 2, iteration(j, j % 2))
            if looped:
                with eng.Fori(0, looped) as b:
                    odd, even = 2 * b + LOOP_FROM, 2 * b + LOOP_FROM + 1
                    steps_of(odd, 1, b + LOOP_FROM // 2, iteration(odd, 1))
                    steps_of(even, 0, b + LOOP_FROM // 2 + 1, iteration(even, 0))
            for j in range(LOOP_FROM + 2 * looped, BLOCKS + 5):
                steps_of(j, j % 2, j // 2, iteration(j, j % 2))

        block = ctx.enter_context(nc.Block())

        @block.sync
        def _(sync):
            sync.dma_start(w_in[:], in_w.rearrange("(k p) n -> p k n", p=P)).then_inc(weights_loaded, 16)
            sync.dma_start(w_conv[:], conv_w.rearrange("(k p) n -> p k n", p=P)).then_inc(weights_loaded, 16)
            sync.dma_start(b_conv[:], conv_b).then_inc(weights_loaded, 16)
            sync.dma_start(d_skip[:], d_param).then_inc(weights_loaded, 16)
            sync.dma_start(neg_a[:], a_log.rearrange("(k p) n -> p k n", p=P)).then_inc(weights_loaded, 16)
            sync.dma_start(w_xp[:], xp_w.rearrange("(k p) n -> p k n", p=P)).then_inc(weights_loaded, 16)
            sync.dma_start(w_router[:], router_w.rearrange("(k p) n -> p k n", p=P)).then_inc(weights_loaded, 16)
            sync.dma_start(b_router[:], router_b.rearrange("(a n) -> a n", a=1).to_broadcast([P, E])).then_inc(weights_loaded, 16)
            sync.dma_start(w_out[:], out_w.rearrange("(k p) n -> p k n", p=P)).then_inc(weights_loaded, 16)

            def steps_of(j, half, pair, steps):
                p, r = j + 1, j - 1
                for s in steps:
                    if s[0] == "load_x":
                        q = s[1]
                        if q >= 2:
                            bank_no, before = use_of(j, half, ("norm_T", q - 2))
                            hold(sync, work_full[bank_no], before + 1)
                        elif not isinstance(j, int) or j >= 0:
                            bank_no, before = use_of(j - 1, 1 - half, ("norm_T", q + 2))
                            hold(sync, work_full[bank_no], before + 1)
                        sync.dma_start(xn[:, q % 2, :], x[bass.ds(p * T + q * P, P), :]).then_inc(x_loaded[q % 2], 16)
                    elif s[0] == "load_res":
                        q = s[1]
                        hold(sync, x1_stored[q % 2], 16 * (2 * r + q // 2))
                        hold(sync, stat2_half, r * Q + q - 1)
                        sync.dma_start(x1[:, q % 2, :], x[bass.ds(r * T + q * P, P), :]).then_inc(res_loaded[q % 2], 16)
                    elif s[0] == "store_x1":
                        q = s[1]
                        bank_no, before = use_of(j, half, ("out_project", q))
                        hold(sync, work_free[bank_no], before + 1)
                        sync.dma_start(x1_dram[bass.ds(r * T + q * P, P), :], x1[:, q % 2, :]).then_inc(x1_stored[q % 2], 16)
                    elif s[0] == "load_x1":
                        q = s[1]
                        hold(sync, x1_stored[q % 2], 16 * (2 * r + q // 2 + 1))
                        if q >= 2 or not isinstance(j, int) or j > 1:
                            hold(sync, scattered[q % 2], 16 * TOP * (2 * r + q // 2))
                        sync.dma_start(xn2[:, q % 2, :], x1_dram[bass.ds(r * T + q * P, P), :]).then_inc(x1_loaded[q % 2], 16)
                    elif s[0] == "b_store":
                        bank_no, before = use_of(j, half, ("b_project", 0))
                        hold(sync, work_free[bank_no], before + 1)
                        sync.dma_start(b_dram[1 - half].rearrange("n (a b) -> n a b", a=2), b_rows).then_inc(b_stored, 16)
                    elif s[0] == "load_b":
                        n, of = s[1], j + s[2]
                        hold(sync, b_stored, 16 * (of + 1))
                        hold(sync, u_ready, (of * N + n - ROWS + 1) * C)
                        sync.dma_start(b_ring[:, n % ROWS, :], b_dram[(half + s[2]) % 2, n:n + 1, :].to_broadcast([P, T])).then_inc(b_loaded[n % ROWS], 16)
                    elif s[0] == "rows_load":
                        i = s[1]
                        if i == 0:
                            hold(sync, table_step, (pair - 1 + half) * TABLE_STEPS)
                            for k in range(2):
                                hold(sync, scattered[k], 16 * TOP * SQ // 2 * (pair - 1 + half))
                            if isinstance(j, int) and j == 3:
                                sync.wait_ge(rows_zeroed, 16 * ZERO_LOADS)
                        if i == 0 and (not isinstance(j, int) or j > 3):
                            bank_no, before = use_of(j - 1, 1 - half, ("rows_T", HALF_XT - 1))
                            hold(sync, work_full[bank_no], before + 1)
                        elif i:
                            bank_no, before = use_of(j, half, ("rows_T", i - 1))
                            hold(sync, work_full[bank_no], before + 1)
                        at = i + (1 - half) * HALF_XT
                        row = sync.value_load(tile_row[0:1, at:at + 1], min_val=0, max_val=2 * REGION - P)
                        sync.dma_start(xe[:], row_dram[bass.ds(row, P), :]).then_inc(rows_loaded, 16)
                    elif s[0] == "rows_store":
                        i = s[1]
                        bank_no, before = use_of(j, half, ("expert", i))
                        hold(sync, work_free[bank_no], before + 1)
                        at = i + (1 - half) * HALF_XT
                        region = (pair + half) % 2
                        sync.dma_start(res_dram[bass.ds(region * RESULTS + at * P, P), :], ye[:]).then_inc(rows_stored, 16)
                    elif s[0] == "fetch":
                        q = s[1]
                        hold(sync, stored, 16 * ((j - 5) * Q + q))
                        hold(sync, x1_stored[q % 2], 16 * (2 * (j - 5) + q // 2 + 1))
                        sync.dma_start(x_out[:], x1_dram[bass.ds((j - 5) * T + q * P, P), :]).then_inc(x_out_loaded, 16)
                    elif s[0] == "store":
                        q = s[1]
                        hold(sync, row_added, TOP * ((j - 5) * Q + q + 1))
                        sync.dma_start(out[bass.ds((j - 5) * T + q * P, P), :], x_out[:]).then_inc(stored, 16)
                if isinstance(j, int) and j == -1:
                    sync.dma_start(w_exp[:].rearrange("p e (k n) -> p e k n", k=C),
                                   expert_w.rearrange("e (k p) n -> p e k n", p=P)).then_inc(experts_loaded, 16)

            run(sync, steps_of)
            sync.wait_ge(stored, 16 * BLOCKS * Q)
            sync.wait_ge(rows_stored, 16 * XT * BATCHES)

        @block.gpsimd
        def _(pool):
            nc.gpsimd.memset(ident[:], 0.0).then_inc(const_step, 1)
            nc.gpsimd.memset(earlier[:], 0.0).then_inc(const_step, 1)
            nc.gpsimd.memset(ones[:], 1.0).then_inc(const_step, 1)
            nc.gpsimd.memset(minus_half[:], -0.5).then_inc(const_step, 1)
            nc.gpsimd.memset(minus_one[:], -1.0).then_inc(const_step, 1)
            nc.gpsimd.iota(lane[:], pattern=[[1, E]], base=0, channel_multiplier=0,
                           allow_small_or_imprecise_dtypes=True).then_inc(const_step, 1)
            nc.gpsimd.iota(tile_no[:], pattern=[[1, XT]], base=0, channel_multiplier=0,
                           allow_small_or_imprecise_dtypes=True).then_inc(const_step, 1)
            nc.gpsimd.iota(row_base[:, 0:E], pattern=[[CAP, E]], base=REGION, channel_multiplier=0,
                           allow_small_or_imprecise_dtypes=True).then_inc(const_step, 1)
            nc.gpsimd.iota(row_flip[:, 0:E], pattern=[[2 * CAP, E]], base=REGION, channel_multiplier=0,
                           allow_small_or_imprecise_dtypes=True).then_inc(const_step, 1)
            nc.gpsimd.memset(row_base[:, E:E + 1], float(RESULTS)).then_inc(const_step, 1)
            nc.gpsimd.memset(row_flip[:, E:E + 1], float(RESULTS)).then_inc(const_step, 1)
            pool.wait_ge(const_step, 11)
            nc.gpsimd.affine_select(out=ident[:], in_=ident[:], compare_op=ALU.not_equal, fill=1.0, base=0,
                                    pattern=[[-1, P]], channel_multiplier=1).then_inc(const_step, 1)
            nc.gpsimd.affine_select(out=earlier[:], in_=earlier[:], compare_op=ALU.is_ge, fill=1.0, base=0,
                                    pattern=[[-1, P]], channel_multiplier=1).then_inc(const_step, 1)
            pool.wait_ge(const_step, 13)
            pool.wait_ge(weights_loaded, 16 * WEIGHT_LOADS)

            def steps_of(j, half, pair, steps):
                p, r = j + 1, j - 1
                for s in steps:
                    if s[0] == "norm_rstd":
                        q = s[1]
                        hold(pool, stat_ready, p * Q + q + 1)
                        nc.gpsimd.tensor_scalar(veps[:, q:q + 1], mv[:, q, 1:2], LN_EPS, None, ALU.add).then_inc(veps_ready, 1)
                        pool.wait_ge(veps_ready, p * Q + q + 1)
                        nc.gpsimd.tensor_tensor(out=rstd[:, q:q + 1], in0=veps[:, q:q + 1], in1=minus_half[:], op=ALU.pow).then_inc(rstd_ready, 1)
                    elif s[0] == "u":
                        n, c = s[1], s[2]
                        if c == 0:
                            pool.wait_ge(b_loaded[n % ROWS], 16 * (j * (N // ROWS) + n // ROWS + 1))
                        if n == 0 and c == 0:
                            pool.wait_ge(xc_ready, (j + 1) * C)
                        g = n * C + c
                        wait(pool, scanned, j * N * C + g - UR + 1)
                        nc.gpsimd.tensor_tensor(out=u[:, g % UR, :], in0=xc[:, half, c, :], in1=b_ring[:, n % ROWS, :], op=ALU.mult).then_inc(u_ready, 1)
                        if n == N - 1:
                            if c == 0:
                                wait_used(pool, j - 1, 1 - half, ("c_project", 1))
                            hold(pool, u_ready, (j * N + n) * C + c + 1)
                            nc.gpsimd.tensor_scalar(xc[:, half, c, :], xc[:, half, c, :], d_skip[:, c:c + 1], None, ALU.mult).then_inc(skip_ready, 1)
                    elif s[0] == "y_gate":
                        q = s[1]
                        wait_used(pool, j, half, ("y_T", q))
                        if q == 0:
                            pool.wait_ge(sz_ready, r + 1)
                        nc.gpsimd.tensor_tensor(out=y2[:, :, q * P:(q + 1) * P], in0=y2[:, :, q * P:(q + 1) * P],
                                                in1=sz[:, 1 - half, :, q * P:(q + 1) * P], op=ALU.mult).then_inc(y_gated, 1)
                    elif s[0] == "rstd2":
                        q = s[1]
                        hold(pool, stat2_ready, r * Q + q + 1)
                        nc.gpsimd.tensor_scalar(veps2[:, q:q + 1], mv2[:, q, 1:2], LN_EPS, None, ALU.add).then_inc(veps2_ready, 1)
                        pool.wait_ge(veps2_ready, r * Q + q + 1)
                        nc.gpsimd.tensor_tensor(out=rstd2[:, q:q + 1], in0=veps2[:, q:q + 1], in1=minus_half[:], op=ALU.pow).then_inc(rstd2_ready, 1)
                    elif s[0] == "gate_weights":
                        q = s[1]
                        tile = r * Q + q
                        at = q + (1 - half) * Q
                        if not isinstance(j, int) or tile:
                            hold(pool, rows_ready, tile)
                        if at == 1:
                            nc.gpsimd.tensor_copy(mask_sum[:], mask[:]).then_inc(mask_summed, 1)
                        elif at:
                            nc.gpsimd.tensor_tensor(out=mask_sum[:], in0=mask_sum[:], in1=mask[:], op=ALU.add).then_inc(mask_summed, 1)
                        else:
                            pool.sem_inc(mask_summed, 1)
                        count = [0]

                        def link(ins):
                            count[0] += 1
                            ins.then_inc(weight_step, 1)
                            hold(pool, weight_step, tile * WEIGHT_STEPS + count[0])

                        if at == 0:
                            wait(pool, aged, pair * AGE_STEPS)
                            wait(pool, table_step, pair * TABLE_STEPS)
                        hold(pool, top_ready, tile + 1)
                        link(nc.gpsimd.tensor_scalar(small[:, 0:1], top_prob[:, 0:1], top_prob[:, 1:2], EPS, ALU.add, ALU.add))
                        link(nc.gpsimd.tensor_tensor(out=small[:, 1:2], in0=small[:, 0:1], in1=minus_one[:, 0:1], op=ALU.pow))
                        link(nc.gpsimd.tensor_scalar(small[:, 2:4], top_prob[:, 0:2], small[:, 1:2], None, ALU.mult))
                        link(nc.gpsimd.tensor_tensor(out=small[:, 4:5], in0=small[:, 2:3], in1=small[:, 3:4], op=ALU.add))
                        link(nc.gpsimd.tensor_scalar(small[:, 5:6], small[:, 4:5], EPS, None, ALU.max))
                        link(nc.gpsimd.tensor_tensor(out=small[:, 6:7], in0=small[:, 5:6], in1=minus_one[:, 0:1], op=ALU.pow))
                        nc.gpsimd.tensor_scalar(small[:, 7:8], small[:, 4:5], EPS, 1.0, ALU.mult, ALU.add)
                        nc.gpsimd.tensor_scalar(pick[:, at, 0, :], lane[:], top_lane[:, 0:1], None, ALU.is_equal)
                        link(nc.gpsimd.tensor_scalar(pick[:, at, 1, :], lane[:], top_lane[:, 1:2], None, ALU.is_equal))
                        link(nc.gpsimd.tensor_scalar(weight_of[0][:, at, :], small[:, 2:4], small[:, 6:7], small[:, 7:8], ALU.mult, ALU.mult))
                        link(nc.gpsimd.tensor_tensor(out=mask[:], in0=pick[:, at, 0, :], in1=pick[:, at, 1, :], op=ALU.add))
                        pool.sem_inc(mask_ready, 1)
                        assert count[0] == WEIGHT_STEPS
                    elif s[0] == "scatter":
                        q = s[1]
                        at = q + (1 - half) * Q
                        hold(pool, rows_ready, r * Q + q + 1)
                        if q == 0 and half == 1 and (not isinstance(j, int) or j >= 5):
                            hold(pool, rows_loaded, 16 * HALF_XT * (j - 3))
                        if isinstance(j, int) and j == 1 and q == 0:
                            pool.wait_ge(rows_zeroed, 16 * ZERO_LOADS)
                        for k in range(TOP):
                            nc.gpsimd.indirect_dma_start(row_dram[:, :], bass.IndirectOffsetOnAxis(ap=row_at[:, at, k:k + 1], axis=0),
                                                         xn2[:, q % 2, :], None).then_inc(scattered[q % 2], 16)
                    elif s[0] == "gather":
                        q, k = s[1], s[2]
                        at = q + (1 - half) * Q
                        if q == 0 and k == 0:
                            hold(pool, rows_stored, 16 * XT * (pair - 2 + half))
                            if half == 1:
                                hold(pool, aged, pair * AGE_STEPS)
                                if not isinstance(j, int) or j <= BLOCKS + 1:
                                    hold(pool, table_step, pair * TABLE_STEPS)
                        hold(pool, row_added, TOP * ((j - 5) * Q + q) + k)
                        nc.gpsimd.indirect_dma_start(y_row[:], None, res_dram[:, :],
                                                     bass.IndirectOffsetOnAxis(ap=rows_of[1][:, at, k:k + 1], axis=0)).then_inc(gathered, 16)

            run(pool, steps_of)

        @block.scalar
        def _(act):
            act.wait_ge(weights_loaded, 16 * WEIGHT_LOADS)
            nc.scalar.activation(neg_a[:], neg_a[:], ACT.Exp).then_inc(a_ready, 1)
            act.wait_ge(a_ready, 1)
            nc.scalar.activation(neg_a[:], neg_a[:], ACT.Copy, scale=-1.0).then_inc(a_ready, 1)
            act.wait_ge(a_ready, 2)
            act.wait_ge(zeros_ready, 1)
            zeros = x_out[:].rearrange("p (a d) -> p a d", a=1)
            part = 2 * REGION // (ZERO_LOADS - 1)
            for i in range(ZERO_LOADS - 1):
                nc.scalar.dma_start(row_dram[i * part:(i + 1) * part, :].rearrange("(p a) d -> p a d", p=P),
                                    zeros.to_broadcast([P, part // P, D])).then_inc(rows_zeroed, 16)
            nc.scalar.dma_start(res_dram[RESULTS:, :].rearrange("(p a) d -> p a d", p=P),
                                zeros.to_broadcast([P, XT, D])).then_inc(rows_zeroed, 16)

            def steps_of(j, half, pair, steps):
                p, r = j + 1, j - 1
                for s in steps:
                    if s[0] == "decay":
                        n, c = s[1], s[2]
                        if n == 0 and c == 0:
                            wait_used(act, j - 1, 1 - half, ("dt_project", 0))
                        g = n * C + c
                        wait(act, scanned, j * N * C + g - 1)
                        nc.scalar.activation(decay_bank[g % 2][:], dt[:, half, :], ACT.Exp, scale=neg_a[:, c, n:n + 1]).then_inc(decay_ready, 1)
                    elif s[0] == "norm_evict":
                        q = s[1]
                        ps, free = wait_full(act, j, half, ("norm_T", q))
                        if q == 0 and (not isinstance(j, int) or j > 0):
                            wait_product(act, j, half, ("out_project", Q - 1), ps)
                        nc.scalar.activation(xnT[:, :, q * P:(q + 1) * P], ps[:].rearrange("p (k t) -> p k t", k=C), ACT.Copy).then_inc(free, 1)
                    elif s[0] == "project_evict":
                        m = s[1]
                        ps, free = wait_full(act, j, half, ("project", m))
                        if m < C:
                            wait(act, b_stored, 16 * p)
                            act.wait_ge(edge_ready, p + 1)
                            nc.scalar.activation(xs[:, m, TAPS - 1:], ps[:], ACT.Copy).then_inc(free, 1)
                        else:
                            wait(act, y_gated, (p - 1) * Q)
                            nc.scalar.activation(sz[:, 1 - half, m - C, :], ps[:], ACT.Copy).then_inc(free, 1)
                    elif s[0] == "silu":
                        for c in range(C):
                            act.wait_ge(conv_tap, (p * C + c + 1) * TAPS)
                            nc.scalar.activation(xc[:, 1 - half, c, :], xc[:, 1 - half, c, :], ACT.Silu, bias=b_conv[:, c:c + 1]).then_inc(xc_ready, 1)
                        wait_used(act, j, half, ("project", M - 1))
                        nc.scalar.activation(sz[:, 1 - half], sz[:, 1 - half], ACT.Silu).then_inc(sz_ready, 1)
                    elif s[0] == "dt_exp":
                        ps, _ = wait_full(act, j, half, ("dt_project", 0))
                        nc.scalar.activation(sp, ps[:].rearrange("p (a b) -> p a b", a=2), ACT.Abs).then_inc(sp_step, 1)
                        act.wait_ge(sp_step, p * 3 + 1)
                        nc.scalar.activation(sp, sp, ACT.Exp, scale=-1.0).then_inc(sp_step, 1)
                        act.wait_ge(sp_step, p * 3 + 2)
                        nc.scalar.activation(sp, sp, ACT.Ln, bias=1.0).then_inc(sp_step, 1)
                    elif s[0] == "c_evict":
                        i = s[1]
                        ps, free = wait_full(act, j, half, ("c_project", i))
                        wait(act, summed, (p - 1) * N * Q)
                        nc.scalar.activation(ct[:, 1 - half, 2 * i:2 * i + 2, :], ps[:, 0:2 * N].rearrange("p (q n) -> p q n", q=2), ACT.Copy).then_inc(free, 1)
                    elif s[0] == "norm2_evict":
                        q = s[1]
                        ps, free = wait_full(act, j, half, ("norm2_T", q))
                        if q:
                            wait_product(act, j, half, ("router", q - 1), ps)
                        elif not isinstance(j, int) or j > 1:
                            wait_product(act, j - 1, 1 - half, ("router", Q - 1), ps)
                        nc.scalar.activation(xn2T[:], ps[:].rearrange("p (k t) -> p k t", k=C), ACT.Copy).then_inc(free, 1)
                    elif s[0] == "gate_exp":
                        q = s[1]
                        act.wait_ge(logits_ready, r * Q + q + 1)
                        nc.scalar.activation(prob[:], logit[:], ACT.Exp, bias=neg_top[:], accum_out=prob_sum[:]).then_inc(prob_ready, 1)
                    elif s[0] == "rows_evict":
                        i = s[1]
                        ps, free = wait_full(act, j, half, ("rows_T", i))
                        if i >= 2:
                            wait_product(act, j, half, ("expert", i - 2), ps)
                        elif not isinstance(j, int) or j > 3:
                            wait_product(act, j - 1, 1 - half, ("expert", HALF_XT + i - 2), ps)
                        nc.scalar.activation(xeT[:, i % 2], ps[:].rearrange("p (k t) -> p k t", k=C), ACT.Copy).then_inc(free, 1)
                    elif s[0] == "expert_evict":
                        i = s[1]
                        ps, free = wait_full(act, j, half, ("expert", i))
                        wait(act, rows_stored, 16 * ((j - 3) * HALF_XT + i))
                        nc.scalar.activation(ye[:], ps[:], ACT.Copy).then_inc(free, 1)

            run(act, steps_of)

        @block.vector
        def _(dve):
            nc.vector.memset(x_out[:], 0.0).then_inc(zeros_ready, 1)
            dve.wait_ge(const_step, 13)
            dve.wait_ge(weights_loaded, 16 * WEIGHT_LOADS)

            def steps_of(j, half, pair, steps):
                p, r = j + 1, j - 1
                for s in steps:
                    if s[0] == "scan":
                        n, c = s[1], s[2]
                        g = n * C + c
                        dve.wait_ge(decay_ready, j * N * C + g + 1)
                        dve.wait_ge(u_ready, j * N * C + g + 1)
                        if c == 0:
                            wait(dve, hT_ready, (j * N + n - 1) * Q)
                        first = 0.0
                        if half == 1:
                            if c == 0:
                                dve.wait_ge(h_kept, (j - 1) * (N // 2) + n + 1)
                            first = h_last[:, n, c:c + 1]
                        nc.vector.tensor_tensor_scan(out=h[:, n % 2, c, :], data0=decay_bank[g % 2][:], data1=u[:, g % UR, :],
                                                     initial=first, op0=ALU.mult, op1=ALU.add).then_inc(scanned, 1)
                    elif s[0] == "keep_h" and half == 0:
                        n = s[1]
                        dve.wait_ge(scanned, (j * N + n + 1) * C)
                        nc.vector.tensor_copy(h_last[:, n, :], h[:, n % 2, :, T - 1]).then_inc(h_kept, 1)
                    elif s[0] == "h_sum":
                        m, q, blk = s[1], s[2], s[3]
                        i, ip = j + blk, half if blk == 0 else 1 - half
                        dve.wait_ge(hT_ready, (i * N + m) * Q + q + 1)
                        if m == 0:
                            if q == 0:
                                wait_used(dve, i - 1, 1 - ip, ("c_project", 1))
                            if not isinstance(j, int) or j > 0:
                                wait_product(dve, j, half, ("y_T", q))
                            nc.vector.tensor_scalar(acc[:, q, :], hT_bank[q % 2][:], ct[:, ip, q, m:m + 1], None, ALU.mult).then_inc(summed, 1)
                        else:
                            dve.wait_ge(summed, (i * N + m - 1) * Q + q + 1)
                            nc.vector.scalar_tensor_tensor(out=acc[:, q, :], in0=hT_bank[q % 2][:], scalar=ct[:, ip, q, m:m + 1],
                                                           in1=acc[:, q, :], op0=ALU.mult, op1=ALU.add).then_inc(summed, 1)
                    elif s[0] == "norm_stat":
                        q = s[1]
                        dve.wait_ge(x_loaded[q % 2], 16 * (2 * p + q // 2 + 1))
                        nc.vector.bn_stats(out=stat[:, q, :], in_=xn[:, q % 2, :]).then_inc(stat_half, 1)
                        hold(dve, stat_half, p * Q + q + 1)
                        nc.vector.bn_aggr(out=mv[:, q, :], in_=stat[:, q, :]).then_inc(stat_ready, 1)
                    elif s[0] == "norm_apply":
                        q = s[1]
                        dve.wait_ge(rstd_ready, p * Q + q + 1)
                        nc.vector.tensor_scalar(xn[:, q % 2, :], xn[:, q % 2, :], mv[:, q, 0:1], rstd[:, q:q + 1],
                                                ALU.subtract, ALU.mult).then_inc(xn_ready, 1)
                    elif s[0] == "conv_edge":
                        wait(dve, conv_tap, p * C * TAPS)
                        if half == 1:
                            nc.vector.memset(xs[:, :, 0:TAPS - 1], 0.0).then_inc(edge_ready, 1)
                        else:
                            nc.vector.tensor_copy(xs[:, :, 0:TAPS - 1], xs[:, :, T:T + TAPS - 1]).then_inc(edge_ready, 1)
                    elif s[0] == "conv":
                        c = s[1]
                        wait_used(dve, j, half, ("project", c))
                        dst = xc[:, 1 - half, c, :]
                        nc.vector.tensor_scalar(dst, xs[:, c, 0:T], w_conv[:, c, 0:1], None, ALU.mult).then_inc(conv_tap, 1)
                        for k in range(1, TAPS):
                            dve.wait_ge(conv_tap, (p * C + c) * TAPS + k)
                            nc.vector.scalar_tensor_tensor(out=dst, in0=xs[:, c, k:k + T], scalar=w_conv[:, c, k:k + 1], in1=dst,
                                                           op0=ALU.mult, op1=ALU.add).then_inc(conv_tap, 1)
                    elif s[0] == "dt_plus":
                        ps, free = wait_full(dve, j, half, ("dt_project", 0))
                        dve.wait_ge(sp_step, (p + 1) * 3)
                        wait(dve, decay_ready, (p - 1) * N * C)
                        nc.vector.scalar_tensor_tensor(out=dt[:, 1 - half, :].rearrange("p (a b) -> p a b", a=2),
                                                       in0=ps[:].rearrange("p (a b) -> p a b", a=2), scalar=0.0, in1=sp,
                                                       op0=ALU.max, op1=ALU.add).then_inc(free, 1)
                    elif s[0] == "b_scale":
                        ps, free = wait_full(dve, j, half, ("b_project", 0))
                        wait_used(dve, j, half, ("dt_project", 0))
                        wait(dve, b_stored, 16 * p)
                        nc.vector.tensor_tensor(out=b_rows, in0=ps[0:N, :].rearrange("p (a b) -> p a b", a=2),
                                                in1=dt[0:N, 1 - half, :].rearrange("p (a b) -> p a b", a=2), op=ALU.mult).then_inc(free, 1)
                    elif s[0] == "y_skip":
                        q = s[1]
                        ps, free = wait_full(dve, j, half, ("y_T", q))
                        if q == 0:
                            dve.wait_ge(skip_ready, (r + 1) * C)
                            if not isinstance(j, int) or j < BLOCKS:
                                wait_product(dve, j - 1, 1 - half, ("project", M - 1), ps)
                            else:
                                wait_product(dve, j - 1, 1 - half, ("out_project", Q - 1), ps)
                        nc.vector.tensor_tensor(out=y2[:, :, q * P:(q + 1) * P], in0=ps[:].rearrange("p (k t) -> p k t", k=C),
                                                in1=xc[:, 1 - half, :, q * P:(q + 1) * P], op=ALU.add).then_inc(free, 1)
                    elif s[0] == "residual":
                        q = s[1]
                        ps, free = wait_full(dve, j, half, ("out_project", q))
                        dve.wait_ge(res_loaded[q % 2], 16 * (2 * r + q // 2 + 1))
                        nc.vector.tensor_tensor(out=x1[:, q % 2, :], in0=ps[:], in1=x1[:, q % 2, :], op=ALU.add).then_inc(free, 1)
                        wait_used(dve, j, half, ("out_project", q))
                        nc.vector.bn_stats(out=stat2[:, q, :], in_=x1[:, q % 2, :]).then_inc(stat2_half, 1)
                        hold(dve, stat2_half, r * Q + q + 1)
                        nc.vector.bn_aggr(out=mv2[:, q, :], in_=stat2[:, q, :]).then_inc(stat2_ready, 1)
                    elif s[0] == "norm2":
                        q = s[1]
                        dve.wait_ge(rstd2_ready, r * Q + q + 1)
                        dve.wait_ge(stat2_ready, r * Q + q + 1)
                        dve.wait_ge(x1_loaded[q % 2], 16 * (2 * r + q // 2 + 1))
                        nc.vector.tensor_scalar(xn2[:, q % 2, :], xn2[:, q % 2, :], mv2[:, q, 0:1], rstd2[:, q:q + 1], ALU.subtract, ALU.mult).then_inc(xn2_ready, 1)
                    elif s[0] == "gate_logits":
                        q = s[1]
                        ps, free = wait_full(dve, j, half, ("router", q))
                        nc.vector.tensor_tensor(out=logit[:], in0=ps[:, 0:E], in1=b_router[:], op=ALU.add).then_inc(free, 1)
                        bank_no, before = use_of(j, half, ("router", q))
                        hold(dve, work_free[bank_no], before + 1)
                        base = (r * Q + q) * GATE_STEPS
                        nc.vector.max(top_logit[:], logit[:]).then_inc(gate_step, 1)
                        dve.wait_ge(gate_step, base + 1)
                        nc.vector.tensor_scalar(neg_top[:], top_logit[:, 0:1], -1.0, None, ALU.mult).then_inc(logits_ready, 1)
                    elif s[0] == "gate_top":
                        q = s[1]
                        base = (r * Q + q) * GATE_STEPS
                        dve.wait_ge(prob_ready, r * Q + q + 1)
                        nc.vector.reciprocal(neg_top[:], prob_sum[:]).then_inc(gate_step, 1)
                        dve.wait_ge(gate_step, base + 2)
                        nc.vector.tensor_scalar(prob[:], prob[:], neg_top[:], None, ALU.mult).then_inc(gate_step, 1)
                        wait(dve, mask_ready, r * Q + q)
                        hold(dve, gate_step, base + 3)
                        nc.vector.max(top_prob[:], prob[:]).then_inc(gate_step, 1)
                        hold(dve, gate_step, base + 4)
                        nc.vector.max_index(top_at[:], top_prob[:], prob[:]).then_inc(gate_step, 1)
                        dve.wait_ge(gate_step, base + 5)
                        nc.vector.tensor_copy(top_lane[:], top_at[:, 0:TOP]).then_inc(top_ready, 1)
                    elif s[0] == "row_of":
                        q = s[1]
                        at = q + (1 - half) * Q
                        ps, free = wait_full(dve, j, half, ("rank", q))
                        if at == 0:
                            dve.wait_ge(flipped, pair + 1)
                        if at == SQ - 1:
                            nc.vector.tensor_scalar(fill[:], ps[:, E:2 * E], float(P - 1), None, ALU.add).then_inc(fill_ready, 1)
                            dve.wait_ge(fill_ready, pair)
                        nc.vector.tensor_tensor(out=rank_row[:], in0=ps[:, 0:E], in1=row_base[:, 0:E], op=ALU.add).then_inc(free, 1)
                        wait_used(dve, j, half, ("rank", q))
                        for k in range(TOP):
                            last = nc.vector.tensor_tensor(out=picked_row[:, k, :], in0=pick[:, at, k, :], in1=rank_row[:], op=ALU.mult)
                        last.then_inc(row_step, 1)
                        dve.wait_ge(row_step, r * Q + q + 1)
                        nc.vector.tensor_reduce(row_f32[:, at, :], picked_row[:], AX.X, ALU.add).then_inc(row_summed, 1)
                        dve.wait_ge(row_summed, r * Q + q + 1)
                        nc.vector.tensor_copy(row_at[:, at, :], row_f32[:, at, :]).then_inc(rows_ready, 1)
                    elif s[0] == "slots_age":
                        tiles = min(j - 1, BLOCKS) * Q if isinstance(j, int) else (j - 1) * Q
                        dve.wait_ge(mask_ready, tiles)
                        if not isinstance(j, int) or j > 3:
                            wait(dve, row_added, TOP * (j - 5) * Q)
                            nc.vector.tensor_copy(rows_of[1][:], rows_of[0][:]).then_inc(aged, 1)
                            nc.vector.tensor_copy(weight_of[2][:], weight_of[1][:]).then_inc(aged, 1)
                            dve.wait_ge(aged, (pair - 1) * AGE_STEPS + 2)
                        else:
                            dve.sem_inc(aged, 2)
                        nc.vector.tensor_copy(weight_of[1][:], weight_of[0][:]).then_inc(aged, 1)
                    elif s[0] == "new_sequence":
                        if not isinstance(j, int) or j >= 3:
                            base = (pair - 1) * TABLE_STEPS
                            count = [0]

                            def link(ins):
                                count[0] += 1
                                ins.then_inc(table_step, 1)
                                dve.wait_ge(table_step, base + count[0])

                            dve.wait_ge(fill_ready, pair)
                            link(nc.vector.tensor_scalar(tiles_i[:], fill[:], 7, None, ALU.arith_shift_right))
                            link(nc.vector.tensor_copy(tiles_f[:], tiles_i[:]))
                            link(nc.vector.tensor_tensor_scan(out=tiles_to[:], data0=ones[:, 0:E], data1=tiles_f[:], initial=0.0,
                                                              op0=ALU.mult, op1=ALU.add))
                            link(nc.vector.tensor_tensor(out=shift[:], in0=tiles_to[:], in1=tiles_f[:], op=ALU.subtract))
                            link(nc.vector.scalar_tensor_tensor(out=shift[:], in0=shift[:], scalar=float(P), in1=row_base[:, 0:E],
                                                                op0=ALU.mult, op1=ALU.subtract))
                            link(nc.vector.tensor_tensor(out=token_shift, in0=pick[:],
                                                         in1=shift[:].rearrange("p (a b e) -> p a b e", a=1, b=1).to_broadcast([P, SQ, TOP, E]), op=ALU.mult))
                            link(nc.vector.tensor_reduce(result_f[:], token_shift, AX.X, ALU.add))
                            link(nc.vector.scalar_tensor_tensor(out=result_f[:], in0=result_f[:], scalar=row_base[:, E:E + 1], in1=row_f32[:],
                                                                op0=ALU.add, op1=ALU.add))
                            link(nc.vector.tensor_copy(rows_of[0][:], result_f[:]))
                            if not isinstance(j, int) or j > 3:
                                dve.wait_ge(rows_stored, 16 * HALF_XT * (j - 3))
                            link(nc.vector.tensor_tensor(out=past, in0=tiles_to[0:1, :].rearrange("p (a e) -> p a e", a=1).to_broadcast([1, XT, E]),
                                                         in1=tile_no[:].rearrange("p (i a) -> p i a", a=1).to_broadcast([1, XT, E]), op=ALU.is_le))
                            link(nc.vector.tensor_reduce(expert_f[:], past, AX.X, ALU.add))
                            link(nc.vector.tensor_tensor(out=past, in0=past,
                                                         in1=tiles_f[0:1, :].rearrange("p (a e) -> p a e", a=1).to_broadcast([1, XT, E]), op=ALU.mult))
                            link(nc.vector.tensor_reduce(before_f[:], past, AX.X, ALU.add))
                            link(nc.vector.scalar_tensor_tensor(out=row_f[:], in0=expert_f[:], scalar=float(CAP // P), in1=before_f[:],
                                                                op0=ALU.mult, op1=ALU.subtract))
                            link(nc.vector.tensor_tensor(out=row_f[:], in0=row_f[:], in1=tile_no[:], op=ALU.add))
                            link(nc.vector.tensor_scalar(row_f[:], row_f[:], float(REGION // P - 1), None, ALU.min))
                            link(nc.vector.tensor_scalar(tile_row[:], row_f[:], float(P), row_base[0:1, 0:1], ALU.mult, ALU.add))
                            link(nc.vector.tensor_scalar(tile_expert[:], expert_f[:], float(E - 1), None, ALU.min))
                            nc.vector.tensor_copy(tiles_i[:], fill[:]).then_inc(table_step, 1)
                            dve.wait_ge(table_step, base + TABLE_STEPS)
                            assert count[0] == TABLE_STEPS - 1, count[0]
                        if not isinstance(j, int) or j < BLOCKS:
                            wait(dve, rows_ready, (j - 1) * Q)
                            nc.vector.tensor_tensor(out=row_base[:], in0=row_flip[:], in1=row_base[:], op=ALU.subtract).then_inc(flipped, 1)
                    elif s[0] == "add_row":
                        q, k = s[1], s[2]
                        at = q + (1 - half) * Q
                        done = TOP * ((j - 5) * Q + q) + k
                        if k == 0:
                            dve.wait_ge(x_out_loaded, 16 * ((j - 5) * Q + q + 1))
                        else:
                            dve.wait_ge(row_added, done)
                        dve.wait_ge(gathered, 16 * (done + 1))
                        nc.vector.scalar_tensor_tensor(out=x_out[:], in0=y_row[:], scalar=weight_of[2][:, at, k:k + 1], in1=x_out[:],
                                                       op0=ALU.mult, op1=ALU.add).then_inc(row_added, 1)

            run(dve, steps_of)

        @block.tensor
        def _(pe):
            pe.wait_ge(const_step, 13)
            pe.wait_ge(weights_loaded, 16 * WEIGHT_LOADS)

            def take(j, half, key):
                bank_no, before = use_of(j, half, key)
                wait(pe, work_free[bank_no], before)
                return work_bank[bank_no], work_full[bank_no]

            def product(ps, left, right):
                for k in range(C):
                    last = nc.tensor.matmul(ps, left(k), right(k), start=(k == 0), stop=(k == C - 1))
                return last

            def transposes(ps, tile):
                for k in range(C):
                    last = nc.tensor.transpose(ps[:, k * P:(k + 1) * P], tile(k), ident[:])
                return last

            def steps_of(j, half, pair, steps):
                p, r = j + 1, j - 1
                for s in steps:
                    if s[0] == "h_T":
                        m, q, blk = s[1], s[2], s[3]
                        i = j + blk
                        if q == 0:
                            pe.wait_ge(scanned, (i * N + m + 1) * C)
                        wait(pe, summed, (i * N + m) * Q + q - 1)
                        transposes(hT_bank[q % 2], lambda k: h[:, m % 2, k, q * P:(q + 1) * P]).then_inc(hT_ready, 1)
                    elif s[0] == "norm_T":
                        q = s[1]
                        ps, full = take(j, half, s)
                        pe.wait_ge(xn_ready, p * Q + q + 1)
                        transposes(ps[:], lambda k: xn[:, q % 2, k * P:(k + 1) * P]).then_inc(full, 1)
                    elif s[0] == "project":
                        m = s[1]
                        ps, full = take(j, half, s)
                        if m == 0:
                            for q in range(Q):
                                wait_used(pe, j, half, ("norm_T", q), ps)
                        product(ps[:], lambda k: w_in[:, k, m * P:(m + 1) * P], lambda k: xnT[:, k, :]).then_inc(full, 1)
                    elif s[0] == "dt_project":
                        ps, full = take(j, half, s)
                        pe.wait_ge(xc_ready, (p + 1) * C)
                        product(ps[:], lambda k: w_xp[:, k, 2 * N:2 * N + 1].to_broadcast([P, P]),
                                lambda k: xc[:, 1 - half, k, :]).then_inc(full, 1)
                    elif s[0] == "b_project":
                        ps, full = take(j, half, s)
                        product(ps[0:N, :], lambda k: w_xp[:, k, 0:N], lambda k: xc[:, 1 - half, k, :]).then_inc(full, 1)
                    elif s[0] == "c_project":
                        ps, full = take(j, half, s)
                        for i in range(2):
                            q = 2 * s[1] + i
                            last = product(ps[:, i * N:(i + 1) * N], lambda k: xc[:, 1 - half, k, q * P:(q + 1) * P],
                                           lambda k: w_xp[:, k, N:2 * N])
                        last.then_inc(full, 1)
                    elif s[0] == "y_T":
                        q = s[1]
                        ps, full = take(j, half, s)
                        pe.wait_ge(summed, (r * N + N - 1) * Q + q + 1)
                        transposes(ps[:], lambda k: acc[:, q, k * P:(k + 1) * P]).then_inc(full, 1)
                    elif s[0] == "out_project":
                        q = s[1]
                        ps, full = take(j, half, s)
                        pe.wait_ge(y_gated, r * Q + q + 1)
                        product(ps[:], lambda k: y2[:, k, q * P:(q + 1) * P], lambda k: w_out[:, k, :]).then_inc(full, 1)
                    elif s[0] == "norm2_T":
                        q = s[1]
                        ps, full = take(j, half, s)
                        pe.wait_ge(xn2_ready, r * Q + q + 1)
                        transposes(ps[:], lambda k: xn2[:, q % 2, k * P:(k + 1) * P]).then_inc(full, 1)
                    elif s[0] == "router":
                        q = s[1]
                        ps, full = take(j, half, s)
                        wait_used(pe, j, half, ("norm2_T", q), ps)
                        product(ps[:, 0:E], lambda k: xn2T[:, k, :], lambda k: w_router[:, k, :]).then_inc(full, 1)
                    elif s[0] == "rank":
                        q = s[1]
                        at = q + (1 - half) * Q
                        ps, full = take(j, half, s)
                        pe.wait_ge(mask_ready, r * Q + q + 1)
                        nc.tensor.matmul(ps[:, 0:E], earlier[:], mask[:], start=True, stop=(at == 0))
                        if at:
                            nc.tensor.matmul(ps[:, 0:E], ones[:, 0:1].to_broadcast([P, P]), mask_sum[:], start=False, stop=True)
                        last = nc.tensor.matmul(ps[:, E:2 * E], ones[:, 0:1].to_broadcast([P, P]), mask[:], start=True, stop=(at == 0))
                        if at:
                            last = nc.tensor.matmul(ps[:, E:2 * E], ones[:, 0:1].to_broadcast([P, P]), mask_sum[:], start=False, stop=True)
                        last.then_inc(full, 1)
                    elif s[0] == "rows_T":
                        i = s[1]
                        ps, full = take(j, half, s)
                        pe.wait_ge(rows_loaded, 16 * ((j - 3) * HALF_XT + i + 1))
                        transposes(ps[:], lambda k: xe[:, k * P:(k + 1) * P]).then_inc(full, 1)
                    elif s[0] == "expert":
                        i = s[1]
                        at = i + (1 - half) * HALF_XT
                        if i == 0 and isinstance(j, int):
                            pe.wait_ge(experts_loaded, 16)
                        if i == 0:
                            hold(pe, table_step, (pair - 1 + half) * TABLE_STEPS)
                        expert = pe.value_load(tile_expert[0:1, at:at + 1], min_val=0, max_val=E - 1)
                        ps, full = take(j, half, s)
                        wait_used(pe, j, half, ("rows_T", i), ps)
                        product(ps[:], lambda k: xeT[:, i % 2, k, :],
                                lambda k: w_exp[:, bass.ds(expert, 1), k * D:(k + 1) * D].rearrange("p a n -> p (a n)")).then_inc(full, 1)

            run(pe, steps_of)


_INS = ['x', 'in_w', 'conv_w', 'conv_b', 'xp_w', 'a_log', 'd_param', 'out_w', 'router_w', 'router_b', 'expert_w']


def kernel(**inputs):
    import numpy as _np
    import concourse.bacc as _bacc
    from concourse import mybir as _mybir
    from concourse.bass_utils import run_bass_kernel_spmd as _run

    a = {k: _np.asarray(v) for k, v in inputs.items()}
    shape = a['L0_attn_x'].shape
    given = {
        'x': a['L0_attn_x'].reshape(-1, shape[-1]),
        'in_w': a['L0_attn_in_proj_w'].T,
        'conv_w': a['L0_attn_conv_w'],
        'conv_b': a['L0_attn_conv_b'].reshape(-1, 128).T,
        'xp_w': a['L0_attn_x_proj_w'].T,
        'a_log': a['L0_attn_A_log'],
        'd_param': a['L0_attn_D_param'].reshape(-1, 128).T,
        'out_w': a['L0_attn_out_proj_w'].T,
        'router_w': a['L0_ffn_router_w'].T,
        'router_b': a['L0_ffn_router_b'],
        'expert_w': a['L0_ffn_expert_weights'],
    }
    nc = _bacc.Bacc("TRN2", target_bir_lowering=False, num_devices=1)
    arrays, args = {}, []
    for name in _INS:
        v = _np.ascontiguousarray(given[name])
        arrays[f"in_{name}"] = v
        args.append(nc.dram_tensor(f"in_{name}", v.shape, _mybir.dt.from_np(v.dtype), kind="ExternalInput").ap())
    out = nc.dram_tensor("out", given['x'].shape, _mybir.dt.from_np(given['x'].dtype), kind="ExternalOutput").ap()
    mamba_moe_kernel(nc, *args, out)
    r = _run(nc, [arrays], core_ids=[0])
    return r.results[0]["out"].reshape(shape)
```

```python
import concourse.bass as bass
from concourse import mybir
from contextlib import ExitStack



def mamba_moe_kernel(nc, x, in_w, conv_w, conv_b, xp_w, a_log, d_param, out_w,
                     router_w, router_b, expert_w, out):
    fp32 = mybir.dt.float32
    u32 = mybir.dt.uint32
    i32 = mybir.dt.int32
    AX = mybir.AxisListType
    ALU = mybir.AluOpType
    ACT = mybir.ActivationFunctionType

    P = 128
    TOKENS, D = x.shape
    SEQ = 1024
    T = 512
    Q = T // P
    C = D // P
    N = a_log.shape[1]
    TAPS = conv_w.shape[1]
    E = expert_w.shape[0]
    BLOCKS = TOKENS // T
    BATCHES = TOKENS // SEQ
    LN_EPS = 1e-5
    EPS = 1e-10
    ROWS = 2
    UR = 4
    M = 2 * C
    TOP = 2
    SQ = SEQ // P
    CAP = SEQ
    XT = TOP * SQ + E
    HALF_XT = XT // 2
    REGION = E * CAP
    RESULTS = XT * P

    PLACES = N * C + 3
    COMBINE = {
        "fetch": [7, 24, 32, 46],
        "gather": [12, 14, 19, 30, 33, 41, 45, 52],
        "add_row": [12, 15, 26, 31, 34, 41, 48, 53],
        "store": [21, 31, 45, 58],
    }
    POST = {
        "load_res": [4, 5, 10, 12],
        "y_T": [0, 1, 2, 4],
        "y_skip": [1, 5, 6, 7],
        "y_gate": [4, 6, 7, 10],
        "out_project": [4, 6, 8, 10],
        "residual": [6, 7, 11, 12],
        "rstd2": [7, 14, 14, 37],
        "store_x1": [6, 7, 16, 25],
        "load_x1": [8, 10, 31, 40],
        "norm2": [10, 14, 37, 42],
        "norm2_T": [11, 20, 38, 44],
        "norm2_evict": [14, 23, 39, 46],
        "router": [14, 28, 40, 48],
        "gate_logits": [14, 29, 41, 49],
        "gate_exp": [16, 30, 48, 52],
        "gate_top": [17, 30, 48, 55],
        "gate_weights": [23, 31, 53, 63],
        "rank": [27, 31, 58, 63],
        "row_of": [28, 35, 59, 63],
        "scatter": [30, 38, 63, 66],
    }
    PREP = {
        "load_x": [5, 9, 19, 23],
        "norm_stat": [10, 10, 23, 23],
        "norm_rstd": [15, 15, 26, 26],
        "norm_apply": [15, 18, 26, 26],
        "norm_T": [17, 20, 26, 27],
        "norm_evict": [20, 24, 28, 28],
        "conv_edge": [18],
        "project": [28, 30, 30, 34, 39, 41, 48, 52],
        "project_evict": [30, 31, 32, 38, 43, 46, 50, 56],
        "conv": [30, 31, 31, 32, 32, 38, 43, 46],
        "silu_x": [49],
        "c_project": [49, 50],
        "dt_project": [50],
        "dt_exp": [54],
        "c_evict": [51, 53],
        "b_project": [56],
        "dt_plus": [54],
        "b_scale": [57],
        "b_store": [57],
        "silu_z": [57],
    }
    EXPERTS = {
        "rows_T": [7, 11, 15, 16, 23, 28, 32, 36, 44, 50, 54, 58],
        "rows_load": [6, 10, 12, 15, 21, 23, 28, 33, 37, 49, 50, 56],
        "rows_evict": [10, 14, 15, 19, 24, 31, 36, 38, 47, 55, 57, 61],
        "expert": [12, 15, 17, 23, 24, 32, 40, 47, 55, 59, 60, 64],
        "expert_evict": [15, 17, 20, 25, 27, 36, 44, 49, 57, 60, 64, 65],
        "rows_store": [15, 17, 21, 26, 29, 41, 45, 54, 59, 60, 64, 65],
    }

    PAIRS = [(i, k) for i in range(Q) for k in range(TOP)]
    CHUNKS = [(m,) for m in [0, 1, 2, 3, 4, 5, 6, 7]]
    INDEX = {"gather": PAIRS, "add_row": PAIRS, "conv": PAIRS, "project": CHUNKS, "project_evict": CHUNKS}

    def steps_in(stage):
        return [(at, (kind,) + index) for kind, places in stage.items()
                for index, at in zip(INDEX.get(kind, [(i,) for i in range(len(places))]), places)]

    ROW_ZEROS, RESULT_ZEROS = 32, 6

    def closing_steps(j, first):
        tiles = [[("rows_load", 0), ("rows_load", 1), ("rows_T", 0), ("rows_load", 2), ("rows_evict", 0)]]
        for i in range(HALF_XT):
            tiles += [[("rows_T", i + 1)] * (i + 1 < HALF_XT) + [("rows_load", i + 3)] * (i + 3 < HALF_XT) +
                      [("rows_evict", i + 1)] * (i + 1 < HALF_XT) + [("expert", i), ("expert_evict", i), ("rows_store", i)]]
        fetch = [[("fetch", q), ("gather", q, 0), ("gather", q, 1)] for q in range(Q)] + [[]]
        rows = [fetch[0]] + [[fetch[q + 1][:1], [("add_row", q, 0), ("add_row", q, 1), ("store", q)], fetch[q + 1][1:]] for q in range(Q)]
        rows[1:] = [sum(x, []) for x in rows[1:]]
        steps = list(first)
        for i in range(1 + HALF_XT):
            steps += tiles[i] if j <= BLOCKS + 2 else []
            steps += rows[i // 3] if i % 3 == 0 else []
        return steps

    def iteration(j, half):
        def on(first, last):
            return not isinstance(j, int) or first <= j <= last
        scan, tail = on(0, BLOCKS - 1), on(1, BLOCKS)
        do_prep, do_post = on(-1, BLOCKS - 2), on(1, BLOCKS)
        side = sum([steps_in(x) for x, do in ((COMBINE, on(5, BLOCKS + 4)), (POST, do_post), (PREP, do_prep),
                                              (EXPERTS, on(3, BLOCKS + 2))) if do], [])
        if half == 1:
            side = [(6, ("slots_age", 0))] * on(3, BLOCKS + 3) + [(6, ("new_sequence", 0))] * on(1, BLOCKS + 1) + side
        if isinstance(j, int) and j == 0:
            side = side + [(2 * i + 1, ("zero_rows", i)) for i in range(ROW_ZEROS)]
        if isinstance(j, int) and j == 1:
            side = side + [(24 + 4 * i, ("load_expert", i)) for i in range(E)]
        if isinstance(j, int) and j == 2:
            side = side + [(8 * i + 1, ("zero_results", i)) for i in range(RESULT_ZEROS)]
        if isinstance(j, int) and j > BLOCKS:
            return closing_steps(j, [s for a, s in side if a == 6 and s[0] in ("slots_age", "new_sequence")])
        place = {at: [s for a, s in side if a == at] for at in range(PLACES)}
        assert sum(len(x) for x in place.values()) == len(side)
        steps = []
        for n in range(N):
            m, blk = (N - 1, -1) if n == 0 else (n - 1, 0)
            summing = tail if n == 0 else scan
            if summing:
                steps += [("h_T", m, 0, blk), ("h_T", m, 1, blk)]
            if scan and n + 1 < N:
                steps.append(("load_b", n + 1, 0))
            elif do_prep and n + 1 == N:
                steps.append(("load_b", 0, 1))
            for c in range(C):
                if scan:
                    steps += [("decay", n, c), ("u", n, c), ("scan", n, c)]
                if summing:
                    steps.append(("h_sum", m, c, blk))
                    if c + 2 < Q:
                        steps.append(("h_T", m, c + 2, blk))
                steps += place[n * C + c]
            if scan:
                steps.append(("keep_h", n))
        return steps + sum([place[at] for at in range(N * C, PLACES)], [])

    WORK = 4
    TAKES = {"norm_T": "norm_evict", "project": "project_evict", "dt_project": "dt_plus", "b_project": "b_scale",
             "c_project": "c_evict", "y_T": "y_skip", "out_project": "residual", "norm2_T": "norm2_evict",
             "router": "gate_logits", "rank": "row_of", "rows_T": "rows_evict", "expert": "expert_evict"}
    LOOP_FROM = 7

    def takes(j):
        out, freed = [], set()
        for s in iteration(j, j % 2):
            if s[0] in TAKES:
                if len(out) >= WORK:
                    old = out[-WORK]
                    assert (TAKES[old[0]], old[1]) in freed, (s, old)
                out.append(s)
            freed.add(s[:2])
        return {s: k for k, s in enumerate(out)}

    ORDINAL = {j: takes(j) for j in range(-1, max(BLOCKS + 5, LOOP_FROM + 2))}
    FIRST_USE = {j: sum(len(ORDINAL[i]) for i in range(-1, j)) for j in ORDINAL}
    LOOP_USES = len(ORDINAL[LOOP_FROM]) if BLOCKS > LOOP_FROM + 1 else WORK
    assert LOOP_USES % WORK == 0

    def use_of(j, half, key):
        if isinstance(j, int):
            k = FIRST_USE[j] + ORDINAL[j][key]
            return k % WORK, k // WORK
        at = LOOP_FROM if half == 1 else LOOP_FROM + 1
        k = FIRST_USE[at] + ORDINAL[at][key]
        return k % WORK, (j - at) * (LOOP_USES // WORK) + k // WORK

    ctx = ExitStack()
    with ctx:
        def sb(name, shape, dt=fp32):
            return ctx.enter_context(nc.sbuf_tensor(name, shape, dt))

        def sem(name):
            return ctx.enter_context(nc.semaphore(name))

        w_in = sb("w_in", [P, C, 2 * D])
        w_out = sb("w_out", [P, C, D])
        w_exp = sb("w_exp", [P, E, C * D])
        w_xp = sb("w_xp", [P, C, 2 * N + 1])
        w_router = sb("w_router", [P, C, E])
        b_router = sb("b_router", [P, E])
        w_conv = sb("w_conv", [P, C, TAPS])
        b_conv = sb("b_conv", [P, C])
        d_skip = sb("d_skip", [P, C])
        neg_a = sb("neg_a", [P, C, N])
        ident = sb("ident", [P, P])
        earlier = sb("earlier", [P, P])
        ones = sb("ones", [P, E])
        lane = sb("lane", [P, E])
        tile_no = sb("tile_no", [1, XT])
        minus_half = sb("minus_half", [P, 1])
        minus_one = sb("minus_one", [P, 2])
        xn = sb("xn", [P, 2, D])
        stat = sb("stat", [P, Q, 6])
        mv = sb("mv", [P, Q, 2])
        veps = sb("veps", [P, Q])
        rstd = sb("rstd", [P, Q])
        xs = sb("xs", [P, C, TAPS - 1 + T])
        sp = xs[:, 0:2, TAPS - 1:TAPS - 1 + T // 2]
        b_rows = xs[0:N, 2:4, TAPS - 1:TAPS - 1 + T // 2]
        bt = xs[:, 2, TAPS - 1 + T // 2:TAPS - 1 + T // 2 + Q * N].rearrange("p (q n) -> p q n", q=Q)
        xc = sb("xc", [P, 2, C, T])
        sz = sb("sz", [P, 2, C, T])
        dt = sb("dt", [P, 2, T])
        ct = sb("ct", [P, 2, Q, N])
        b_ring = sb("b_ring", [P, ROWS, T])
        u = sb("u", [P, UR, T])
        h = sb("h", [P, 2, C, T])
        h_last = sb("h_last", [P, N, C])
        acc = sb("acc", [P, Q, D])
        y2 = sb("y2", [P, C, T])
        xnT = y2
        x1 = sb("x1", [P, 2, D])
        stat2 = sb("stat2", [P, Q, 6])
        mv2 = sb("mv2", [P, Q, 2])
        veps2 = sb("veps2", [P, Q])
        rstd2 = sb("rstd2", [P, Q])
        xn2 = sb("xn2", [P, 2, D])
        xn2T = sb("xn2T", [P, C, P])
        logit = sb("logit", [P, E])
        top_logit = sb("top_logit", [P, 8])
        neg_top = sb("neg_top", [P, 1])
        prob = sb("prob", [P, E])
        prob_sum = sb("prob_sum", [P, 1])
        top_prob = sb("top_prob", [P, 8])
        top_at = sb("top_at", [P, 8], u32)
        top_lane = sb("top_lane", [P, TOP])
        small = sb("small", [P, 8])
        pick = sb("pick", [P, SQ, TOP, E])
        mask = sb("mask", [P, E])
        mask_sum = sb("mask_sum", [P, E])
        row_base = sb("row_base", [P, E + 1])
        row_flip = sb("row_flip", [P, E + 1])
        rank_row = sb("rank_row", [P, E])
        picked_row = sb("picked_row", [P, TOP, E])
        row_f32 = sb("row_f32", [P, SQ, TOP])
        row_at = sb("row_at", [P, SQ, TOP], u32)
        rows_of = [sb(f"rows_of{i}", [P, SQ, TOP], u32) for i in range(2)]
        weight_of = [sb(f"weight_of{i}", [P, SQ, TOP]) for i in range(3)]
        fill = sb("fill", [P, E], i32)
        tiles_i = sb("tiles_i", [P, E], i32)
        tiles_f = sb("tiles_f", [P, E])
        tiles_to = sb("tiles_to", [P, E])
        shift = sb("shift", [P, E])
        result_f = sb("result_f", [P, SQ, TOP])
        expert_f = sb("expert_f", [1, XT])
        before_f = sb("before_f", [1, XT])
        row_f = sb("row_f", [1, XT])
        tile_row = sb("tile_row", [1, XT], i32)
        tile_expert = sb("tile_expert", [1, XT], i32)
        xe = sb("xe", [P, D])
        xeT = sb("xeT", [P, 2, C, P])
        ye = sb("ye", [P, D])
        x_out = sb("x_out", [P, D])
        y_row = sb("y_row", [P, D])
        token_shift = y_row[:, 0:SQ * TOP * E].rearrange("p (t k e) -> p t k e", t=SQ, k=TOP)
        past = y_row[0:1, SQ * TOP * E:SQ * TOP * E + XT * E].rearrange("p (i e) -> p i e", i=XT)

        def bank(name):
            return ctx.enter_context(nc.psum_tensor(name, [P, 512], fp32))

        decay_bank = [bank(f"decay{i}") for i in range(2)]
        hT_bank = [bank(f"hT{i}") for i in range(2)]
        work_bank = [bank(f"work{i}") for i in range(WORK)]

        b_dram = nc.dram_tensor("b_scratch", [2, N, T], fp32, kind="Internal").ap()
        x1_dram = nc.dram_tensor("x1_scratch", [TOKENS, D], fp32, kind="Internal").ap()
        row_dram = nc.dram_tensor("row_scratch", [2 * REGION, D], fp32, kind="Internal").ap()
        res_dram = nc.dram_tensor("result_scratch", [2 * RESULTS, D], fp32, kind="Internal").ap()

        work_full = [sem(f"work_full{i}") for i in range(WORK)]
        work_free = [sem(f"work_free{i}") for i in range(WORK)]
        weights_loaded = sem("weights_loaded")
        experts_loaded = sem("experts_loaded")
        const_step = sem("const_step")
        rows_zeroed = sem("rows_zeroed")
        results_zeroed = sem("results_zeroed")
        zeros_ready = sem("zeros_ready")
        a_ready = sem("a_ready")
        x_loaded = [sem(f"x_loaded{i}") for i in range(2)]
        stat_half = sem("stat_half")
        stat_ready = sem("stat_ready")
        veps_ready = sem("veps_ready")
        rstd_ready = sem("rstd_ready")
        xn_ready = sem("xn_ready")
        edge_ready = sem("edge_ready")
        conv_tap = sem("conv_tap")
        xc_ready = sem("xc_ready")
        sz_ready = sem("sz_ready")
        sp_step = sem("sp_step")
        b_stored = sem("b_stored")
        b_loaded = [sem(f"b_loaded{i}") for i in range(ROWS)]
        skip_ready = sem("skip_ready")
        u_ready = sem("u_ready")
        decay_ready = sem("decay_ready")
        scanned = sem("scanned")
        h_kept = sem("h_kept")
        hT_ready = sem("hT_ready")
        summed = sem("summed")
        y_gated = sem("y_gated")
        res_loaded = [sem(f"res_loaded{i}") for i in range(2)]
        x1_loaded = [sem(f"x1_loaded{i}") for i in range(2)]
        x1_stored = [sem(f"x1_stored{i}") for i in range(2)]
        stat2_half = sem("stat2_half")
        stat2_ready = sem("stat2_ready")
        veps2_ready = sem("veps2_ready")
        rstd2_ready = sem("rstd2_ready")
        xn2_ready = sem("xn2_ready")
        gate_step = sem("gate_step")
        logits_ready = sem("logits_ready")
        prob_ready = sem("prob_ready")
        top_ready = sem("top_ready")
        mask_summed = sem("mask_summed")
        weight_step = sem("weight_step")
        mask_ready = sem("mask_ready")
        fill_ready = sem("fill_ready")
        row_step = sem("row_step")
        row_summed = sem("row_summed")
        rows_ready = sem("rows_ready")
        scattered = [sem(f"scattered{i}") for i in range(2)]
        aged = sem("aged")
        flipped = sem("flipped")
        table_step = sem("table_step")
        rows_loaded = [sem(f"rows_loaded{i}") for i in range(2)]
        rows_stored = [sem(f"rows_stored{i}") for i in range(2)]
        gathered = [sem(f"gathered{i}") for i in range(2)]
        x_out_loaded = [sem(f"x_out_loaded{i}") for i in range(2)]
        row_added = sem("row_added")
        stored = [sem(f"stored{i}") for i in range(2)]

        GATE_STEPS, WEIGHT_STEPS, TABLE_STEPS, AGE_STEPS = 5, 9, 19, 3
        WEIGHT_LOADS = 9

        def wait(eng, s, value):
            if not isinstance(value, int) or value > 0:
                eng.wait_ge(s, value)

        def hold(eng, s, value):
            wait(eng, s, value)
            eng.nop(nofuse=True)

        def closing(j):
            return isinstance(j, int) and j > BLOCKS

        def xe_of(j, i):
            return xn[:, 0, :] if closing(j) and i % 2 else xe[:]

        def ye_of(j, i):
            return xn[:, 1, :] if closing(j) and i % 2 else ye[:]

        def x_out_of(j, q):
            return x1[:, 0, :] if closing(j) and q % 2 else x_out[:]

        def y_row_of(j, k):
            return xn2[:, 0, :] if closing(j) and k else y_row[:]

        def wait_full(eng, j, half, key):
            bank_no, before = use_of(j, half, key)
            eng.wait_ge(work_full[bank_no], before + 1)
            return work_bank[bank_no], work_free[bank_no]

        def wait_product(eng, j, half, key, ps=None):
            bank_no, before = use_of(j, half, key)
            if work_bank[bank_no] is not ps:
                eng.wait_ge(work_full[bank_no], before + 1)

        def wait_used(eng, j, half, key, ps=None):
            bank_no, before = use_of(j, half, key)
            if work_bank[bank_no] is not ps:
                eng.wait_ge(work_free[bank_no], before + 1)

        def run(eng, steps_of):
            looped = max(BLOCKS - LOOP_FROM - 1, 0) // 2
            for j in range(-1, LOOP_FROM):
                steps_of(j, j % 2, j // 2, iteration(j, j % 2))
            if looped:
                with eng.Fori(0, looped) as b:
                    odd, even = 2 * b + LOOP_FROM, 2 * b + LOOP_FROM + 1
                    steps_of(odd, 1, b + LOOP_FROM // 2, iteration(odd, 1))
                    steps_of(even, 0, b + LOOP_FROM // 2 + 1, iteration(even, 0))
            for j in range(LOOP_FROM + 2 * looped, BLOCKS + 5):
                steps_of(j, j % 2, j // 2, iteration(j, j % 2))

        block = ctx.enter_context(nc.Block())

        @block.sync
        def _(sync):
            sync.dma_start(w_in[:], in_w.rearrange("(k p) n -> p k n", p=P)).then_inc(weights_loaded, 16)
            sync.dma_start(w_conv[:], conv_w.rearrange("(k p) n -> p k n", p=P)).then_inc(weights_loaded, 16)
            sync.dma_start(b_conv[:], conv_b).then_inc(weights_loaded, 16)
            sync.dma_start(d_skip[:], d_param).then_inc(weights_loaded, 16)
            sync.dma_start(neg_a[:], a_log.rearrange("(k p) n -> p k n", p=P)).then_inc(weights_loaded, 16)
            sync.dma_start(w_xp[:], xp_w.rearrange("(k p) n -> p k n", p=P)).then_inc(weights_loaded, 16)
            sync.dma_start(w_router[:], router_w.rearrange("(k p) n -> p k n", p=P)).then_inc(weights_loaded, 16)
            sync.dma_start(b_router[:], router_b.rearrange("(a n) -> a n", a=1).to_broadcast([P, E])).then_inc(weights_loaded, 16)
            sync.dma_start(w_out[:], out_w.rearrange("(k p) n -> p k n", p=P)).then_inc(weights_loaded, 16)

            def steps_of(j, half, pair, steps):
                p, r = j + 1, j - 1
                for s in steps:
                    if s[0] == "load_x":
                        q = s[1]
                        if q >= 2:
                            bank_no, before = use_of(j, half, ("norm_T", q - 2))
                            hold(sync, work_full[bank_no], before + 1)
                        elif not isinstance(j, int) or j >= 0:
                            bank_no, before = use_of(j - 1, 1 - half, ("norm_T", q + 2))
                            hold(sync, work_full[bank_no], before + 1)
                        sync.dma_start(xn[:, q % 2, :], x[bass.ds(p * T + q * P, P), :]).then_inc(x_loaded[q % 2], 16)
                    elif s[0] == "load_res":
                        q = s[1]
                        hold(sync, x1_stored[q % 2], 16 * (2 * r + q // 2))
                        hold(sync, stat2_half, r * Q + q - 1)
                        sync.dma_start(x1[:, q % 2, :], x[bass.ds(r * T + q * P, P), :]).then_inc(res_loaded[q % 2], 16)
                    elif s[0] == "store_x1":
                        q = s[1]
                        bank_no, before = use_of(j, half, ("out_project", q))
                        hold(sync, work_free[bank_no], before + 1)
                        sync.dma_start(x1_dram[bass.ds(r * T + q * P, P), :], x1[:, q % 2, :]).then_inc(x1_stored[q % 2], 16)
                    elif s[0] == "load_expert":
                        sync.dma_start(w_exp[:, s[1]].rearrange("p (k n) -> p k n", k=C),
                                       expert_w[s[1]].rearrange("(k p) n -> p k n", p=P)).then_inc(experts_loaded, 16)
                    elif s[0] == "load_x1":
                        q = s[1]
                        hold(sync, x1_stored[q % 2], 16 * (2 * r + q // 2 + 1))
                        if q >= 2 or not isinstance(j, int) or j > 1:
                            hold(sync, scattered[q % 2], 16 * TOP * (2 * r + q // 2))
                        sync.dma_start(xn2[:, q % 2, :], x1_dram[bass.ds(r * T + q * P, P), :]).then_inc(x1_loaded[q % 2], 16)
                    elif s[0] == "b_store":
                        bank_no, before = use_of(j, half, ("b_project", 0))
                        hold(sync, work_free[bank_no], before + 1)
                        sync.dma_start(b_dram[1 - half].rearrange("n (a b) -> n a b", a=2), b_rows).then_inc(b_stored, 16)
                    elif s[0] == "load_b":
                        n, of = s[1], j + s[2]
                        hold(sync, b_stored, 16 * (of + 1))
                        hold(sync, u_ready, (of * N + n - ROWS + 1) * C)
                        sync.dma_start(b_ring[:, n % ROWS, :], b_dram[(half + s[2]) % 2, n:n + 1, :].to_broadcast([P, T])).then_inc(b_loaded[n % ROWS], 16)
                    elif s[0] == "rows_load":
                        i = s[1]
                        if i == 0:
                            hold(sync, table_step, (pair - 1 + half) * TABLE_STEPS)
                            for k in range(2):
                                hold(sync, scattered[k], 16 * TOP * SQ // 2 * (pair - 1 + half))
                            if isinstance(j, int) and j == 3:
                                sync.wait_ge(rows_zeroed, 16 * ROW_ZEROS)
                                sync.wait_ge(results_zeroed, 16 * RESULT_ZEROS)
                        slots = 2 if closing(j) else 1
                        if i == 0 and (not isinstance(j, int) or j > 3):
                            bank_no, before = use_of(j - 1, 1 - half, ("rows_T", HALF_XT - 1))
                            hold(sync, work_full[bank_no], before + 1)
                        elif i >= slots:
                            bank_no, before = use_of(j, half, ("rows_T", i - slots))
                            hold(sync, work_full[bank_no], before + 1)
                        elif i and j == BLOCKS + 1:
                            bank_no, before = use_of(BLOCKS - 2, 0, ("norm_T", Q - 1))
                            hold(sync, work_full[bank_no], before + 1)
                        at = i + (1 - half) * HALF_XT
                        row = sync.value_load(tile_row[0:1, at:at + 1], min_val=0, max_val=2 * REGION - P)
                        sync.dma_start(xe_of(j, i), row_dram[bass.ds(row, P), :]).then_inc(rows_loaded[i % 2], 16)
                    elif s[0] == "rows_store":
                        i = s[1]
                        bank_no, before = use_of(j, half, ("expert", i))
                        hold(sync, work_free[bank_no], before + 1)
                        at = i + (1 - half) * HALF_XT
                        region = (pair + half) % 2
                        sync.dma_start(res_dram[bass.ds(region * RESULTS + at * P, P), :], ye_of(j, i)).then_inc(rows_stored[i % 2], 16)
                    elif s[0] == "fetch":
                        q = s[1]
                        if closing(j):
                            hold(sync, stored[q % 2], 16 * (2 * (j - 5) + q // 2))
                        if not closing(j) or q == 0:
                            hold(sync, stored[(q + 1) % 2], 16 * (2 * (j - 5) + (q + 1) // 2))
                        elif j == BLOCKS + 1 and q == 1:
                            hold(sync, stat2_half, BLOCKS * Q)
                            hold(sync, x1_stored[0], 16 * 2 * BLOCKS)
                        hold(sync, x1_stored[q % 2], 16 * (2 * (j - 5) + q // 2 + 1))
                        sync.dma_start(x_out_of(j, q), x1_dram[bass.ds((j - 5) * T + q * P, P), :]).then_inc(x_out_loaded[q % 2], 16)
                    elif s[0] == "store":
                        q = s[1]
                        hold(sync, row_added, TOP * ((j - 5) * Q + q + 1))
                        sync.dma_start(out[bass.ds((j - 5) * T + q * P, P), :], x_out_of(j, q)).then_inc(stored[q % 2], 16)

            run(sync, steps_of)
            for k in range(2):
                sync.wait_ge(stored[k], 16 * BLOCKS * Q // 2)
                sync.wait_ge(rows_stored[k], 16 * XT // 2 * BATCHES)

        @block.gpsimd
        def _(pool):
            nc.gpsimd.memset(ident[:], 0.0).then_inc(const_step, 1)
            nc.gpsimd.memset(earlier[:], 0.0).then_inc(const_step, 1)
            nc.gpsimd.memset(ones[:], 1.0).then_inc(const_step, 1)
            nc.gpsimd.memset(minus_half[:], -0.5).then_inc(const_step, 1)
            nc.gpsimd.memset(minus_one[:], -1.0).then_inc(const_step, 1)
            nc.gpsimd.iota(lane[:], pattern=[[1, E]], base=0, channel_multiplier=0,
                           allow_small_or_imprecise_dtypes=True).then_inc(const_step, 1)
            nc.gpsimd.iota(tile_no[:], pattern=[[1, XT]], base=0, channel_multiplier=0,
                           allow_small_or_imprecise_dtypes=True).then_inc(const_step, 1)
            nc.gpsimd.iota(row_base[:, 0:E], pattern=[[CAP, E]], base=REGION, channel_multiplier=0,
                           allow_small_or_imprecise_dtypes=True).then_inc(const_step, 1)
            nc.gpsimd.iota(row_flip[:, 0:E], pattern=[[2 * CAP, E]], base=REGION, channel_multiplier=0,
                           allow_small_or_imprecise_dtypes=True).then_inc(const_step, 1)
            nc.gpsimd.memset(row_base[:, E:E + 1], float(RESULTS)).then_inc(const_step, 1)
            nc.gpsimd.memset(row_flip[:, E:E + 1], float(RESULTS)).then_inc(const_step, 1)
            pool.wait_ge(const_step, 11)
            nc.gpsimd.affine_select(out=ident[:], in_=ident[:], compare_op=ALU.not_equal, fill=1.0, base=0,
                                    pattern=[[-1, P]], channel_multiplier=1).then_inc(const_step, 1)
            nc.gpsimd.affine_select(out=earlier[:], in_=earlier[:], compare_op=ALU.is_ge, fill=1.0, base=0,
                                    pattern=[[-1, P]], channel_multiplier=1).then_inc(const_step, 1)
            pool.wait_ge(const_step, 13)
            pool.wait_ge(weights_loaded, 16 * WEIGHT_LOADS)

            def steps_of(j, half, pair, steps):
                p, r = j + 1, j - 1
                for s in steps:
                    if s[0] == "norm_rstd":
                        q = s[1]
                        hold(pool, stat_ready, p * Q + q + 1)
                        nc.gpsimd.tensor_scalar(veps[:, q:q + 1], mv[:, q, 1:2], LN_EPS, None, ALU.add).then_inc(veps_ready, 1)
                        pool.wait_ge(veps_ready, p * Q + q + 1)
                        nc.gpsimd.tensor_tensor(out=rstd[:, q:q + 1], in0=veps[:, q:q + 1], in1=minus_half[:], op=ALU.pow).then_inc(rstd_ready, 1)
                    elif s[0] == "u":
                        n, c = s[1], s[2]
                        if c == 0:
                            pool.wait_ge(b_loaded[n % ROWS], 16 * (j * (N // ROWS) + n // ROWS + 1))
                        if n == 0 and c == 0:
                            pool.wait_ge(xc_ready, (j + 1) * C)
                        g = n * C + c
                        wait(pool, scanned, j * N * C + g - UR + 1)
                        nc.gpsimd.tensor_tensor(out=u[:, g % UR, :], in0=xc[:, half, c, :], in1=b_ring[:, n % ROWS, :], op=ALU.mult).then_inc(u_ready, 1)
                        if n == N - 1:
                            if c == 0:
                                wait_used(pool, j - 1, 1 - half, ("c_project", 1))
                            hold(pool, u_ready, (j * N + n) * C + c + 1)
                            nc.gpsimd.tensor_scalar(xc[:, half, c, :], xc[:, half, c, :], d_skip[:, c:c + 1], None, ALU.mult).then_inc(skip_ready, 1)
                    elif s[0] == "y_gate":
                        q = s[1]
                        wait_used(pool, j, half, ("y_T", q))
                        if q == 0:
                            pool.wait_ge(sz_ready, r + 1)
                        nc.gpsimd.tensor_tensor(out=y2[:, :, q * P:(q + 1) * P], in0=y2[:, :, q * P:(q + 1) * P],
                                                in1=sz[:, 1 - half, :, q * P:(q + 1) * P], op=ALU.mult).then_inc(y_gated, 1)
                    elif s[0] == "rstd2":
                        q = s[1]
                        hold(pool, stat2_ready, r * Q + q + 1)
                        nc.gpsimd.tensor_scalar(veps2[:, q:q + 1], mv2[:, q, 1:2], LN_EPS, None, ALU.add).then_inc(veps2_ready, 1)
                        pool.wait_ge(veps2_ready, r * Q + q + 1)
                        nc.gpsimd.tensor_tensor(out=rstd2[:, q:q + 1], in0=veps2[:, q:q + 1], in1=minus_half[:], op=ALU.pow).then_inc(rstd2_ready, 1)
                    elif s[0] == "gate_weights":
                        q = s[1]
                        tile = r * Q + q
                        at = q + (1 - half) * Q
                        if not isinstance(j, int) or tile:
                            hold(pool, rows_ready, tile)
                        if at == 1:
                            nc.gpsimd.tensor_copy(mask_sum[:], mask[:]).then_inc(mask_summed, 1)
                        elif at:
                            nc.gpsimd.tensor_tensor(out=mask_sum[:], in0=mask_sum[:], in1=mask[:], op=ALU.add).then_inc(mask_summed, 1)
                        else:
                            pool.sem_inc(mask_summed, 1)
                        count = [0]

                        def link(ins):
                            count[0] += 1
                            ins.then_inc(weight_step, 1)
                            hold(pool, weight_step, tile * WEIGHT_STEPS + count[0])

                        if at == 0:
                            wait(pool, aged, pair * AGE_STEPS)
                            wait(pool, table_step, pair * TABLE_STEPS)
                        hold(pool, top_ready, tile + 1)
                        link(nc.gpsimd.tensor_scalar(small[:, 0:1], top_prob[:, 0:1], top_prob[:, 1:2], EPS, ALU.add, ALU.add))
                        link(nc.gpsimd.tensor_tensor(out=small[:, 1:2], in0=small[:, 0:1], in1=minus_one[:, 0:1], op=ALU.pow))
                        link(nc.gpsimd.tensor_scalar(small[:, 2:4], top_prob[:, 0:2], small[:, 1:2], None, ALU.mult))
                        link(nc.gpsimd.tensor_tensor(out=small[:, 4:5], in0=small[:, 2:3], in1=small[:, 3:4], op=ALU.add))
                        link(nc.gpsimd.tensor_scalar(small[:, 5:6], small[:, 4:5], EPS, None, ALU.max))
                        link(nc.gpsimd.tensor_tensor(out=small[:, 6:7], in0=small[:, 5:6], in1=minus_one[:, 0:1], op=ALU.pow))
                        nc.gpsimd.tensor_scalar(small[:, 7:8], small[:, 4:5], EPS, 1.0, ALU.mult, ALU.add)
                        nc.gpsimd.tensor_scalar(pick[:, at, 0, :], lane[:], top_lane[:, 0:1], None, ALU.is_equal)
                        link(nc.gpsimd.tensor_scalar(pick[:, at, 1, :], lane[:], top_lane[:, 1:2], None, ALU.is_equal))
                        link(nc.gpsimd.tensor_scalar(weight_of[0][:, at, :], small[:, 2:4], small[:, 6:7], small[:, 7:8], ALU.mult, ALU.mult))
                        link(nc.gpsimd.tensor_tensor(out=mask[:], in0=pick[:, at, 0, :], in1=pick[:, at, 1, :], op=ALU.add))
                        pool.sem_inc(mask_ready, 1)
                        assert count[0] == WEIGHT_STEPS
                    elif s[0] == "scatter":
                        q = s[1]
                        at = q + (1 - half) * Q
                        hold(pool, rows_ready, r * Q + q + 1)
                        if q == 0 and half == 1 and (not isinstance(j, int) or j >= 5):
                            for k in range(2):
                                hold(pool, rows_loaded[k], 16 * HALF_XT // 2 * (j - 3))
                        if isinstance(j, int) and j == 1 and q == 0:
                            pool.wait_ge(rows_zeroed, 16 * ROW_ZEROS)
                        for k in range(TOP):
                            nc.gpsimd.indirect_dma_start(row_dram[:, :], bass.IndirectOffsetOnAxis(ap=row_at[:, at, k:k + 1], axis=0),
                                                         xn2[:, q % 2, :], None).then_inc(scattered[q % 2], 16)
                    elif s[0] == "gather":
                        q, k = s[1], s[2]
                        at = q + (1 - half) * Q
                        if q == 0 and k == 0:
                            for i in range(2):
                                hold(pool, rows_stored[i], 16 * XT // 2 * (pair - 2 + half))
                            if half == 1:
                                hold(pool, aged, pair * AGE_STEPS)
                                if not isinstance(j, int) or j <= BLOCKS + 1:
                                    hold(pool, table_step, pair * TABLE_STEPS)
                        if not closing(j):
                            hold(pool, row_added, TOP * ((j - 5) * Q + q) + k)
                        elif q == 0:
                            hold(pool, row_added, TOP * (j - 5) * Q)
                            if j == BLOCKS + 1 and k == 1:
                                hold(pool, scattered[0], 16 * TOP * 2 * BLOCKS)
                        else:
                            hold(pool, row_added, TOP * ((j - 5) * Q + q - 1) + k + 1)
                        nc.gpsimd.indirect_dma_start(y_row_of(j, k), None, res_dram[:, :],
                                                     bass.IndirectOffsetOnAxis(ap=rows_of[1][:, at, k:k + 1], axis=0)).then_inc(gathered[k], 16)

            run(pool, steps_of)

        @block.scalar
        def _(act):
            act.wait_ge(weights_loaded, 16 * WEIGHT_LOADS)
            nc.scalar.activation(neg_a[:], neg_a[:], ACT.Exp).then_inc(a_ready, 1)
            act.wait_ge(a_ready, 1)
            nc.scalar.activation(neg_a[:], neg_a[:], ACT.Copy, scale=-1.0).then_inc(a_ready, 1)
            act.wait_ge(a_ready, 2)
            act.wait_ge(zeros_ready, 1)
            zeros = x_out[:].rearrange("p (a d) -> p a d", a=1)

            def steps_of(j, half, pair, steps):
                p, r = j + 1, j - 1
                for s in steps:
                    if s[0] == "zero_rows":
                        part = 2 * REGION // ROW_ZEROS
                        nc.scalar.dma_start(row_dram[s[1] * part:(s[1] + 1) * part, :].rearrange("(p a) d -> p a d", p=P),
                                            zeros.to_broadcast([P, part // P, D])).then_inc(rows_zeroed, 16)
                    elif s[0] == "zero_results":
                        part = RESULTS // RESULT_ZEROS
                        nc.scalar.dma_start(res_dram[RESULTS + s[1] * part:RESULTS + (s[1] + 1) * part, :].rearrange("(p a) d -> p a d", p=P),
                                            zeros.to_broadcast([P, part // P, D])).then_inc(results_zeroed, 16)
                    elif s[0] == "decay":
                        n, c = s[1], s[2]
                        if n == 0 and c == 0:
                            wait_used(act, j - 1, 1 - half, ("dt_project", 0))
                        g = n * C + c
                        wait(act, scanned, j * N * C + g - 1)
                        nc.scalar.activation(decay_bank[g % 2][:], dt[:, half, :], ACT.Exp, scale=neg_a[:, c, n:n + 1]).then_inc(decay_ready, 1)
                    elif s[0] == "norm_evict":
                        q = s[1]
                        ps, free = wait_full(act, j, half, ("norm_T", q))
                        if q == 0 and (not isinstance(j, int) or j > 0):
                            wait_product(act, j, half, ("out_project", Q - 1), ps)
                        nc.scalar.activation(xnT[:, :, q * P:(q + 1) * P], ps[:].rearrange("p (k t) -> p k t", k=C), ACT.Copy).then_inc(free, 1)
                    elif s[0] == "project_evict":
                        m = s[1]
                        ps, free = wait_full(act, j, half, ("project", m))
                        if m < C:
                            wait(act, b_stored, 16 * p)
                            act.wait_ge(edge_ready, p + 1)
                            nc.scalar.activation(xs[:, m, TAPS - 1:], ps[:], ACT.Copy).then_inc(free, 1)
                        else:
                            wait(act, y_gated, (p - 1) * Q)
                            nc.scalar.activation(sz[:, 1 - half, m - C, :], ps[:], ACT.Copy).then_inc(free, 1)
                    elif s[0] == "silu_x":
                        for c in range(C):
                            act.wait_ge(conv_tap, (p * C + c + 1) * TAPS)
                            nc.scalar.activation(xc[:, 1 - half, c, :], xc[:, 1 - half, c, :], ACT.Silu, bias=b_conv[:, c:c + 1]).then_inc(xc_ready, 1)
                    elif s[0] == "silu_z":
                        wait_used(act, j, half, ("project", M - 1))
                        nc.scalar.activation(sz[:, 1 - half], sz[:, 1 - half], ACT.Silu).then_inc(sz_ready, 1)
                    elif s[0] == "dt_exp":
                        ps, _ = wait_full(act, j, half, ("dt_project", 0))
                        nc.scalar.activation(sp, ps[:].rearrange("p (a b) -> p a b", a=2), ACT.Abs).then_inc(sp_step, 1)
                        act.wait_ge(sp_step, p * 3 + 1)
                        nc.scalar.activation(sp, sp, ACT.Exp, scale=-1.0).then_inc(sp_step, 1)
                        act.wait_ge(sp_step, p * 3 + 2)
                        nc.scalar.activation(sp, sp, ACT.Ln, bias=1.0).then_inc(sp_step, 1)
                    elif s[0] == "c_evict":
                        i = s[1]
                        ps, free = wait_full(act, j, half, ("c_project", i))
                        wait(act, summed, (p - 1) * N * Q)
                        both = ps[:, 0:4 * N].rearrange("p (q n) -> p q n", q=2)
                        nc.scalar.activation(bt[:, 2 * i:2 * i + 2, :], both[:, :, 0:N], ACT.Copy)
                        nc.scalar.activation(ct[:, 1 - half, 2 * i:2 * i + 2, :], both[:, :, N:2 * N], ACT.Copy).then_inc(free, 1)
                    elif s[0] == "norm2_evict":
                        q = s[1]
                        ps, free = wait_full(act, j, half, ("norm2_T", q))
                        if q:
                            wait_product(act, j, half, ("router", q - 1), ps)
                        elif not isinstance(j, int) or j > 1:
                            wait_product(act, j - 1, 1 - half, ("router", Q - 1), ps)
                        nc.scalar.activation(xn2T[:], ps[:].rearrange("p (k t) -> p k t", k=C), ACT.Copy).then_inc(free, 1)
                    elif s[0] == "gate_exp":
                        q = s[1]
                        act.wait_ge(logits_ready, r * Q + q + 1)
                        nc.scalar.activation(prob[:], logit[:], ACT.Exp, bias=neg_top[:], accum_out=prob_sum[:]).then_inc(prob_ready, 1)
                    elif s[0] == "rows_evict":
                        i = s[1]
                        ps, free = wait_full(act, j, half, ("rows_T", i))
                        if i >= 2:
                            wait_product(act, j, half, ("expert", i - 2), ps)
                        elif not isinstance(j, int) or j > 3:
                            wait_product(act, j - 1, 1 - half, ("expert", HALF_XT + i - 2), ps)
                        nc.scalar.activation(xeT[:, i % 2], ps[:].rearrange("p (k t) -> p k t", k=C), ACT.Copy).then_inc(free, 1)
                    elif s[0] == "expert_evict":
                        i = s[1]
                        ps, free = wait_full(act, j, half, ("expert", i))
                        if closing(j):
                            act.wait_ge(rows_stored[i % 2], 16 * ((j - 3) * HALF_XT // 2 + i // 2))
                        if not closing(j) or i == 0:
                            wait(act, rows_stored[(i + 1) % 2], 16 * ((j - 3) * (HALF_XT // 2) + (i + 1) // 2))
                        nc.scalar.activation(ye_of(j, i), ps[:], ACT.Copy).then_inc(free, 1)

            run(act, steps_of)

        @block.vector
        def _(dve):
            nc.vector.memset(x_out[:], 0.0).then_inc(zeros_ready, 1)
            dve.wait_ge(const_step, 13)
            dve.wait_ge(weights_loaded, 16 * WEIGHT_LOADS)

            def steps_of(j, half, pair, steps):
                p, r = j + 1, j - 1
                for s in steps:
                    if s[0] == "scan":
                        n, c = s[1], s[2]
                        g = n * C + c
                        dve.wait_ge(decay_ready, j * N * C + g + 1)
                        dve.wait_ge(u_ready, j * N * C + g + 1)
                        if c == 0:
                            wait(dve, hT_ready, (j * N + n - 1) * Q)
                        first = 0.0
                        if half == 1:
                            if c == 0:
                                dve.wait_ge(h_kept, (j - 1) * (N // 2) + n + 1)
                            first = h_last[:, n, c:c + 1]
                        nc.vector.tensor_tensor_scan(out=h[:, n % 2, c, :], data0=decay_bank[g % 2][:], data1=u[:, g % UR, :],
                                                     initial=first, op0=ALU.mult, op1=ALU.add).then_inc(scanned, 1)
                    elif s[0] == "keep_h" and half == 0:
                        n = s[1]
                        dve.wait_ge(scanned, (j * N + n + 1) * C)
                        nc.vector.tensor_copy(h_last[:, n, :], h[:, n % 2, :, T - 1]).then_inc(h_kept, 1)
                    elif s[0] == "h_sum":
                        m, q, blk = s[1], s[2], s[3]
                        i, ip = j + blk, half if blk == 0 else 1 - half
                        dve.wait_ge(hT_ready, (i * N + m) * Q + q + 1)
                        if m == 0:
                            if q == 0:
                                wait_used(dve, i - 1, 1 - ip, ("c_project", 1))
                            if not isinstance(j, int) or j > 0:
                                wait_product(dve, j, half, ("y_T", q))
                            nc.vector.tensor_scalar(acc[:, q, :], hT_bank[q % 2][:], ct[:, ip, q, m:m + 1], None, ALU.mult).then_inc(summed, 1)
                        else:
                            dve.wait_ge(summed, (i * N + m - 1) * Q + q + 1)
                            nc.vector.scalar_tensor_tensor(out=acc[:, q, :], in0=hT_bank[q % 2][:], scalar=ct[:, ip, q, m:m + 1],
                                                           in1=acc[:, q, :], op0=ALU.mult, op1=ALU.add).then_inc(summed, 1)
                    elif s[0] == "norm_stat":
                        q = s[1]
                        dve.wait_ge(x_loaded[q % 2], 16 * (2 * p + q // 2 + 1))
                        nc.vector.bn_stats(out=stat[:, q, :], in_=xn[:, q % 2, :]).then_inc(stat_half, 1)
                        hold(dve, stat_half, p * Q + q + 1)
                        nc.vector.bn_aggr(out=mv[:, q, :], in_=stat[:, q, :]).then_inc(stat_ready, 1)
                    elif s[0] == "norm_apply":
                        q = s[1]
                        dve.wait_ge(rstd_ready, p * Q + q + 1)
                        nc.vector.tensor_scalar(xn[:, q % 2, :], xn[:, q % 2, :], mv[:, q, 0:1], rstd[:, q:q + 1],
                                                ALU.subtract, ALU.mult).then_inc(xn_ready, 1)
                    elif s[0] == "conv_edge":
                        wait(dve, conv_tap, p * C * TAPS)
                        if half == 1:
                            nc.vector.memset(xs[:, :, 0:TAPS - 1], 0.0).then_inc(edge_ready, 1)
                        else:
                            nc.vector.tensor_copy(xs[:, :, 0:TAPS - 1], xs[:, :, T:T + TAPS - 1]).then_inc(edge_ready, 1)
                    elif s[0] == "conv":
                        c = s[1]
                        dst = xc[:, 1 - half, c, :]
                        if s[2] == 0:
                            wait_used(dve, j, half, ("project", c))
                            nc.vector.tensor_scalar(dst, xs[:, c, 0:T], w_conv[:, c, 0:1], None, ALU.mult).then_inc(conv_tap, 1)
                        for k in (range(1, TAPS // 2) if s[2] == 0 else range(TAPS // 2, TAPS)):
                            dve.wait_ge(conv_tap, (p * C + c) * TAPS + k)
                            nc.vector.scalar_tensor_tensor(out=dst, in0=xs[:, c, k:k + T], scalar=w_conv[:, c, k:k + 1], in1=dst,
                                                           op0=ALU.mult, op1=ALU.add).then_inc(conv_tap, 1)
                    elif s[0] == "dt_plus":
                        ps, free = wait_full(dve, j, half, ("dt_project", 0))
                        dve.wait_ge(sp_step, (p + 1) * 3)
                        wait(dve, decay_ready, (p - 1) * N * C)
                        nc.vector.scalar_tensor_tensor(out=dt[:, 1 - half, :].rearrange("p (a b) -> p a b", a=2),
                                                       in0=ps[:].rearrange("p (a b) -> p a b", a=2), scalar=0.0, in1=sp,
                                                       op0=ALU.max, op1=ALU.add).then_inc(free, 1)
                    elif s[0] == "b_scale":
                        ps, free = wait_full(dve, j, half, ("b_project", 0))
                        wait_used(dve, j, half, ("dt_project", 0))
                        wait(dve, b_stored, 16 * p)
                        nc.vector.tensor_tensor(out=b_rows, in0=ps[0:N, :].rearrange("p (a b) -> p a b", a=2),
                                                in1=dt[0:N, 1 - half, :].rearrange("p (a b) -> p a b", a=2), op=ALU.mult).then_inc(free, 1)
                    elif s[0] == "y_skip":
                        q = s[1]
                        ps, free = wait_full(dve, j, half, ("y_T", q))
                        if q == 0:
                            dve.wait_ge(skip_ready, (r + 1) * C)
                            if not isinstance(j, int) or j < BLOCKS:
                                wait_product(dve, j - 1, 1 - half, ("project", M - 1), ps)
                            else:
                                wait_product(dve, j - 1, 1 - half, ("out_project", Q - 1), ps)
                        nc.vector.tensor_tensor(out=y2[:, :, q * P:(q + 1) * P], in0=ps[:].rearrange("p (k t) -> p k t", k=C),
                                                in1=xc[:, 1 - half, :, q * P:(q + 1) * P], op=ALU.add).then_inc(free, 1)
                    elif s[0] == "residual":
                        q = s[1]
                        ps, free = wait_full(dve, j, half, ("out_project", q))
                        dve.wait_ge(res_loaded[q % 2], 16 * (2 * r + q // 2 + 1))
                        nc.vector.tensor_tensor(out=x1[:, q % 2, :], in0=ps[:], in1=x1[:, q % 2, :], op=ALU.add).then_inc(free, 1)
                        wait_used(dve, j, half, ("out_project", q))
                        nc.vector.bn_stats(out=stat2[:, q, :], in_=x1[:, q % 2, :]).then_inc(stat2_half, 1)
                        hold(dve, stat2_half, r * Q + q + 1)
                        nc.vector.bn_aggr(out=mv2[:, q, :], in_=stat2[:, q, :]).then_inc(stat2_ready, 1)
                    elif s[0] == "norm2":
                        q = s[1]
                        dve.wait_ge(rstd2_ready, r * Q + q + 1)
                        dve.wait_ge(stat2_ready, r * Q + q + 1)
                        dve.wait_ge(x1_loaded[q % 2], 16 * (2 * r + q // 2 + 1))
                        nc.vector.tensor_scalar(xn2[:, q % 2, :], xn2[:, q % 2, :], mv2[:, q, 0:1], rstd2[:, q:q + 1], ALU.subtract, ALU.mult).then_inc(xn2_ready, 1)
                    elif s[0] == "gate_logits":
                        q = s[1]
                        ps, free = wait_full(dve, j, half, ("router", q))
                        nc.vector.tensor_tensor(out=logit[:], in0=ps[:, 0:E], in1=b_router[:], op=ALU.add).then_inc(free, 1)
                        bank_no, before = use_of(j, half, ("router", q))
                        hold(dve, work_free[bank_no], before + 1)
                        base = (r * Q + q) * GATE_STEPS
                        nc.vector.max(top_logit[:], logit[:]).then_inc(gate_step, 1)
                        dve.wait_ge(gate_step, base + 1)
                        nc.vector.tensor_scalar(neg_top[:], top_logit[:, 0:1], -1.0, None, ALU.mult).then_inc(logits_ready, 1)
                    elif s[0] == "gate_top":
                        q = s[1]
                        base = (r * Q + q) * GATE_STEPS
                        dve.wait_ge(prob_ready, r * Q + q + 1)
                        nc.vector.reciprocal(neg_top[:], prob_sum[:]).then_inc(gate_step, 1)
                        dve.wait_ge(gate_step, base + 2)
                        nc.vector.tensor_scalar(prob[:], prob[:], neg_top[:], None, ALU.mult).then_inc(gate_step, 1)
                        wait(dve, mask_ready, r * Q + q)
                        hold(dve, gate_step, base + 3)
                        nc.vector.max(top_prob[:], prob[:]).then_inc(gate_step, 1)
                        hold(dve, gate_step, base + 4)
                        nc.vector.max_index(top_at[:], top_prob[:], prob[:]).then_inc(gate_step, 1)
                        dve.wait_ge(gate_step, base + 5)
                        nc.vector.tensor_copy(top_lane[:], top_at[:, 0:TOP]).then_inc(top_ready, 1)
                    elif s[0] == "row_of":
                        q = s[1]
                        at = q + (1 - half) * Q
                        ps, free = wait_full(dve, j, half, ("rank", q))
                        if at == 0:
                            dve.wait_ge(flipped, pair + 1)
                        if at == SQ - 1:
                            nc.vector.tensor_scalar(fill[:], ps[:, E:2 * E], float(P - 1), None, ALU.add).then_inc(fill_ready, 1)
                            dve.wait_ge(fill_ready, pair)
                        nc.vector.tensor_tensor(out=rank_row[:], in0=ps[:, 0:E], in1=row_base[:, 0:E], op=ALU.add).then_inc(free, 1)
                        wait_used(dve, j, half, ("rank", q))
                        for k in range(TOP):
                            last = nc.vector.tensor_tensor(out=picked_row[:, k, :], in0=pick[:, at, k, :], in1=rank_row[:], op=ALU.mult)
                        last.then_inc(row_step, 1)
                        dve.wait_ge(row_step, r * Q + q + 1)
                        nc.vector.tensor_reduce(row_f32[:, at, :], picked_row[:], AX.X, ALU.add).then_inc(row_summed, 1)
                        dve.wait_ge(row_summed, r * Q + q + 1)
                        nc.vector.tensor_copy(row_at[:, at, :], row_f32[:, at, :]).then_inc(rows_ready, 1)
                    elif s[0] == "slots_age":
                        tiles = min(j - 1, BLOCKS) * Q if isinstance(j, int) else (j - 1) * Q
                        dve.wait_ge(mask_ready, tiles)
                        if not isinstance(j, int) or j > 3:
                            wait(dve, row_added, TOP * (j - 5) * Q)
                            nc.vector.tensor_copy(rows_of[1][:], rows_of[0][:]).then_inc(aged, 1)
                            nc.vector.tensor_copy(weight_of[2][:], weight_of[1][:]).then_inc(aged, 1)
                            dve.wait_ge(aged, (pair - 1) * AGE_STEPS + 2)
                        else:
                            dve.sem_inc(aged, 2)
                        nc.vector.tensor_copy(weight_of[1][:], weight_of[0][:]).then_inc(aged, 1)
                    elif s[0] == "new_sequence":
                        if not isinstance(j, int) or j >= 3:
                            base = (pair - 1) * TABLE_STEPS
                            count = [0]

                            def link(ins):
                                count[0] += 1
                                ins.then_inc(table_step, 1)
                                dve.wait_ge(table_step, base + count[0])

                            dve.wait_ge(fill_ready, pair)
                            link(nc.vector.tensor_scalar(tiles_i[:], fill[:], 7, None, ALU.arith_shift_right))
                            link(nc.vector.tensor_copy(tiles_f[:], tiles_i[:]))
                            link(nc.vector.tensor_tensor_scan(out=tiles_to[:], data0=ones[:, 0:E], data1=tiles_f[:], initial=0.0,
                                                              op0=ALU.mult, op1=ALU.add))
                            link(nc.vector.tensor_tensor(out=shift[:], in0=tiles_to[:], in1=tiles_f[:], op=ALU.subtract))
                            link(nc.vector.scalar_tensor_tensor(out=shift[:], in0=shift[:], scalar=float(P), in1=row_base[:, 0:E],
                                                                op0=ALU.mult, op1=ALU.subtract))
                            link(nc.vector.tensor_tensor(out=token_shift, in0=pick[:],
                                                         in1=shift[:].rearrange("p (a b e) -> p a b e", a=1, b=1).to_broadcast([P, SQ, TOP, E]), op=ALU.mult))
                            link(nc.vector.tensor_reduce(result_f[:], token_shift, AX.X, ALU.add))
                            link(nc.vector.scalar_tensor_tensor(out=result_f[:], in0=result_f[:], scalar=row_base[:, E:E + 1], in1=row_f32[:],
                                                                op0=ALU.add, op1=ALU.add))
                            link(nc.vector.tensor_copy(rows_of[0][:], result_f[:]))
                            if not isinstance(j, int) or j > 3:
                                for k in range(2):
                                    dve.wait_ge(rows_stored[k], 16 * HALF_XT // 2 * (j - 3))
                            link(nc.vector.tensor_tensor(out=past, in0=tiles_to[0:1, :].rearrange("p (a e) -> p a e", a=1).to_broadcast([1, XT, E]),
                                                         in1=tile_no[:].rearrange("p (i a) -> p i a", a=1).to_broadcast([1, XT, E]), op=ALU.is_le))
                            link(nc.vector.tensor_reduce(expert_f[:], past, AX.X, ALU.add))
                            link(nc.vector.tensor_tensor(out=past, in0=past,
                                                         in1=tiles_f[0:1, :].rearrange("p (a e) -> p a e", a=1).to_broadcast([1, XT, E]), op=ALU.mult))
                            link(nc.vector.tensor_reduce(before_f[:], past, AX.X, ALU.add))
                            link(nc.vector.scalar_tensor_tensor(out=row_f[:], in0=expert_f[:], scalar=float(CAP // P), in1=before_f[:],
                                                                op0=ALU.mult, op1=ALU.subtract))
                            link(nc.vector.tensor_tensor(out=row_f[:], in0=row_f[:], in1=tile_no[:], op=ALU.add))
                            link(nc.vector.tensor_scalar(row_f[:], row_f[:], float(REGION // P - 1), None, ALU.min))
                            link(nc.vector.tensor_scalar(tile_row[:], row_f[:], float(P), row_base[0:1, 0:1], ALU.mult, ALU.add))
                            link(nc.vector.tensor_scalar(tile_expert[:], expert_f[:], float(E - 1), None, ALU.min))
                            nc.vector.tensor_copy(tiles_i[:], fill[:]).then_inc(table_step, 1)
                            dve.wait_ge(table_step, base + TABLE_STEPS)
                            assert count[0] == TABLE_STEPS - 1, count[0]
                        if not isinstance(j, int) or j < BLOCKS:
                            wait(dve, rows_ready, (j - 1) * Q)
                            nc.vector.tensor_tensor(out=row_base[:], in0=row_flip[:], in1=row_base[:], op=ALU.subtract).then_inc(flipped, 1)
                    elif s[0] == "add_row":
                        q, k = s[1], s[2]
                        at = q + (1 - half) * Q
                        done = TOP * ((j - 5) * Q + q) + k
                        if k == 0:
                            dve.wait_ge(x_out_loaded[q % 2], 16 * (2 * (j - 5) + q // 2 + 1))
                        else:
                            dve.wait_ge(row_added, done)
                        dve.wait_ge(gathered[k], 16 * ((j - 5) * Q + q + 1))
                        x_row = x_out_of(j, q)
                        nc.vector.scalar_tensor_tensor(out=x_row, in0=y_row_of(j, k), scalar=weight_of[2][:, at, k:k + 1], in1=x_row,
                                                       op0=ALU.mult, op1=ALU.add).then_inc(row_added, 1)

            run(dve, steps_of)

        @block.tensor
        def _(pe):
            pe.wait_ge(const_step, 13)
            pe.wait_ge(weights_loaded, 16 * WEIGHT_LOADS)

            def take(j, half, key):
                bank_no, before = use_of(j, half, key)
                wait(pe, work_free[bank_no], before)
                return work_bank[bank_no], work_full[bank_no]

            def product(ps, left, right):
                for k in range(C):
                    last = nc.tensor.matmul(ps, left(k), right(k), start=(k == 0), stop=(k == C - 1))
                return last

            def transposes(ps, tile):
                for k in range(C):
                    last = nc.tensor.transpose(ps[:, k * P:(k + 1) * P], tile(k), ident[:])
                return last

            def steps_of(j, half, pair, steps):
                p, r = j + 1, j - 1
                for s in steps:
                    if s[0] == "h_T":
                        m, q, blk = s[1], s[2], s[3]
                        i = j + blk
                        if q == 0:
                            pe.wait_ge(scanned, (i * N + m + 1) * C)
                        wait(pe, summed, (i * N + m) * Q + q - 1)
                        transposes(hT_bank[q % 2], lambda k: h[:, m % 2, k, q * P:(q + 1) * P]).then_inc(hT_ready, 1)
                    elif s[0] == "norm_T":
                        q = s[1]
                        ps, full = take(j, half, s)
                        pe.wait_ge(xn_ready, p * Q + q + 1)
                        transposes(ps[:], lambda k: xn[:, q % 2, k * P:(k + 1) * P]).then_inc(full, 1)
                    elif s[0] == "project":
                        m = s[1]
                        ps, full = take(j, half, s)
                        if m == 0:
                            wait_used(pe, j, half, ("norm_T", Q - 1), ps)
                        product(ps[:], lambda k: w_in[:, k, m * P:(m + 1) * P], lambda k: xnT[:, k, :]).then_inc(full, 1)
                    elif s[0] == "dt_project":
                        ps, full = take(j, half, s)
                        pe.wait_ge(xc_ready, (p + 1) * C)
                        product(ps[:], lambda k: w_xp[:, k, 2 * N:2 * N + 1].to_broadcast([P, P]),
                                lambda k: xc[:, 1 - half, k, :]).then_inc(full, 1)
                    elif s[0] == "b_project":
                        ps, full = take(j, half, s)
                        wait_used(pe, j, half, ("c_project", 1), ps)
                        for q in range(Q):
                            last = nc.tensor.transpose(ps[0:N, q * P:(q + 1) * P], bt[:, q, :], ident[:])
                        last.then_inc(full, 1)
                    elif s[0] == "c_project":
                        pe.wait_ge(xc_ready, (p + 1) * C)
                        ps, full = take(j, half, s)
                        for i in range(2):
                            q = 2 * s[1] + i
                            last = product(ps[:, i * 2 * N:(i + 1) * 2 * N], lambda k: xc[:, 1 - half, k, q * P:(q + 1) * P],
                                           lambda k: w_xp[:, k, 0:2 * N])
                        last.then_inc(full, 1)
                    elif s[0] == "y_T":
                        q = s[1]
                        ps, full = take(j, half, s)
                        pe.wait_ge(summed, (r * N + N - 1) * Q + q + 1)
                        transposes(ps[:], lambda k: acc[:, q, k * P:(k + 1) * P]).then_inc(full, 1)
                    elif s[0] == "out_project":
                        q = s[1]
                        ps, full = take(j, half, s)
                        pe.wait_ge(y_gated, r * Q + q + 1)
                        product(ps[:], lambda k: y2[:, k, q * P:(q + 1) * P], lambda k: w_out[:, k, :]).then_inc(full, 1)
                    elif s[0] == "norm2_T":
                        q = s[1]
                        ps, full = take(j, half, s)
                        pe.wait_ge(xn2_ready, r * Q + q + 1)
                        transposes(ps[:], lambda k: xn2[:, q % 2, k * P:(k + 1) * P]).then_inc(full, 1)
                    elif s[0] == "router":
                        q = s[1]
                        ps, full = take(j, half, s)
                        wait_used(pe, j, half, ("norm2_T", q), ps)
                        product(ps[:, 0:E], lambda k: xn2T[:, k, :], lambda k: w_router[:, k, :]).then_inc(full, 1)
                    elif s[0] == "rank":
                        q = s[1]
                        at = q + (1 - half) * Q
                        ps, full = take(j, half, s)
                        pe.wait_ge(mask_ready, r * Q + q + 1)
                        nc.tensor.matmul(ps[:, 0:E], earlier[:], mask[:], start=True, stop=(at == 0))
                        if at:
                            nc.tensor.matmul(ps[:, 0:E], ones[:, 0:1].to_broadcast([P, P]), mask_sum[:], start=False, stop=True)
                        last = nc.tensor.matmul(ps[:, E:2 * E], ones[:, 0:1].to_broadcast([P, P]), mask[:], start=True, stop=(at == 0))
                        if at:
                            last = nc.tensor.matmul(ps[:, E:2 * E], ones[:, 0:1].to_broadcast([P, P]), mask_sum[:], start=False, stop=True)
                        last.then_inc(full, 1)
                    elif s[0] == "rows_T":
                        i = s[1]
                        ps, full = take(j, half, s)
                        pe.wait_ge(rows_loaded[i % 2], 16 * ((j - 3) * (HALF_XT // 2) + i // 2 + 1))
                        transposes(ps[:], lambda k: xe_of(j, i)[:, k * P:(k + 1) * P]).then_inc(full, 1)
                    elif s[0] == "expert":
                        i = s[1]
                        at = i + (1 - half) * HALF_XT
                        if i == 0 and isinstance(j, int):
                            pe.wait_ge(experts_loaded, 16 * E)
                        if i == 0:
                            hold(pe, table_step, (pair - 1 + half) * TABLE_STEPS)
                        expert = pe.value_load(tile_expert[0:1, at:at + 1], min_val=0, max_val=E - 1)
                        ps, full = take(j, half, s)
                        wait_used(pe, j, half, ("rows_T", i), ps)
                        product(ps[:], lambda k: xeT[:, i % 2, k, :],
                                lambda k: w_exp[:, bass.ds(expert, 1), k * D:(k + 1) * D].rearrange("p a n -> p (a n)")).then_inc(full, 1)

            run(pe, steps_of)


_INS = ['x', 'in_w', 'conv_w', 'conv_b', 'xp_w', 'a_log', 'd_param', 'out_w', 'router_w', 'router_b', 'expert_w']


def kernel(**inputs):
    import numpy as _np
    import concourse.bacc as _bacc
    from concourse import mybir as _mybir
    from concourse.bass_utils import run_bass_kernel_spmd as _run

    a = {k: _np.asarray(v) for k, v in inputs.items()}
    shape = a['L0_attn_x'].shape
    given = {
        'x': a['L0_attn_x'].reshape(-1, shape[-1]),
        'in_w': a['L0_attn_in_proj_w'].T,
        'conv_w': a['L0_attn_conv_w'],
        'conv_b': a['L0_attn_conv_b'].reshape(-1, 128).T,
        'xp_w': a['L0_attn_x_proj_w'].T,
        'a_log': a['L0_attn_A_log'],
        'd_param': a['L0_attn_D_param'].reshape(-1, 128).T,
        'out_w': a['L0_attn_out_proj_w'].T,
        'router_w': a['L0_ffn_router_w'].T,
        'router_b': a['L0_ffn_router_b'],
        'expert_w': a['L0_ffn_expert_weights'],
    }
    nc = _bacc.Bacc("TRN2", target_bir_lowering=False, num_devices=1)
    arrays, args = {}, []
    for name in _INS:
        v = _np.ascontiguousarray(given[name])
        arrays[f"in_{name}"] = v
        args.append(nc.dram_tensor(f"in_{name}", v.shape, _mybir.dt.from_np(v.dtype), kind="ExternalInput").ap())
    out = nc.dram_tensor("out", given['x'].shape, _mybir.dt.from_np(given['x'].dtype), kind="ExternalOutput").ap()
    mamba_moe_kernel(nc, *args, out)
    r = _run(nc, [arrays], core_ids=[0])
    return r.results[0]["out"].reshape(shape)
```
